# Optimizing a Trainium2 kernel written in Bass

```python
import numpy as np
import jax
import jax.numpy as jnp

def _softmax(x, axis=-1):
    return jax.nn.softmax(x, axis=axis)

def _gelu(x):
    return jax.nn.gelu(x, approximate=True)

def _silu(x):
    return jax.nn.silu(x)

def _sigmoid(x):
    return jax.nn.sigmoid(x)

def _layernorm(x, axis=-1, eps=1e-05):
    m = jnp.mean(x, axis=axis, keepdims=True)
    v = jnp.var(x, axis=axis, keepdims=True)
    return (x - m) / jnp.sqrt(v + eps)

def _scatter_add(tgt, idx, src, axis=0):
    return tgt.at[idx].add(src)

def _segment_sum(src, seg, n):
    return jax.ops.segment_sum(src, seg, n)
kernel_name = 'mk_adaln_ffn_d2_seqx_r8_3b3c16'

def setup_inputs(seed: int=0):
    np.random.seed(seed)
    _w = jnp.asarray

    def _rec_inputs():
        import jax
        import jax.numpy as jnp
        _rk = jax.random.key(seed)
        x = -7.109e-05 + 0.9999 * jax.random.normal(jax.random.fold_in(_rk, 1), (32, 32, 256), jnp.float32)
        _lenS = 32 - jax.random.randint(jax.random.fold_in(_rk, 7), (32,), 0, max(1, 32 // 4) + 1, jnp.int32)
        _lenS2 = 32 - jax.random.randint(jax.random.fold_in(_rk, 8), (32,), 0, max(1, 32 // 4) + 1, jnp.int32)
        itok_B_0_7 = jax.random.randint(jax.random.fold_in(_rk, 11), (32,), 0, 8, jnp.int32)
        return (x, itok_B_0_7)
    x, itok_B_0_7 = _rec_inputs()

    def _L0_cond_setup():
        import jax, jax.numpy as jnp
        import numpy as np
        B, C, D, T, N_SUBJECTS = (128, 32, 32, 256, 8)
        key = jax.random.key(seed)
        kx, ks, kw = jax.random.split(key, 3)
        x = jax.random.normal(kx, (B, C, T), dtype=jnp.float32)
        subjects = jax.random.randint(ks, (B,), 0, N_SUBJECTS, dtype=jnp.int64)
        weights = jax.random.normal(kw, (N_SUBJECTS, C, D), dtype=jnp.float32) * (1.0 / C ** 0.5)
        return {'x': x, 'subjects': subjects, 'weights': weights}
    _L0_cond_all = _L0_cond_setup()
    _L0_cond_in = {k: v for k, v in _L0_cond_all.items() if k in ('weights',)}
    del _L0_cond_all

    def _L0_ffn_setup():
        import jax, jax.numpy as jnp
        import numpy as np
        E = 8
        CAPACITY_FACTOR = 1.25
        B, T, H, I = (4, 128, 256, 176)
        key = jax.random.key(seed)
        k0, k1, k2, k3, k4 = jax.random.split(key, 5)
        x = jax.random.normal(k0, (B, T, H), jnp.float32)
        Wr = jax.random.normal(k1, (E, H), jnp.float32) * 0.02
        Wg = jax.random.normal(k2, (E, I, H), jnp.float32) * 0.02
        Wu = jax.random.normal(k3, (E, I, H), jnp.float32) * 0.02
        Wd = jax.random.normal(k4, (E, H, I), jnp.float32) * 0.02
        return {'x': x, 'Wr': Wr, 'Wg': Wg, 'Wu': Wu, 'Wd': Wd}
    _L0_ffn_all = _L0_ffn_setup()
    _L0_ffn_in = {k: v for k, v in _L0_ffn_all.items() if k in ('Wr', 'Wg', 'Wu', 'Wd')}
    del _L0_ffn_all

    def _L1_cond_setup():
        import jax, jax.numpy as jnp
        import numpy as np

        def _lora_linear(x, W, A, B, adapter_indices):
            base = jnp.einsum('bsd,df->bsf', x, W)
            Ai = A[adapter_indices]
            Bi = B[adapter_indices]
            lora = jnp.einsum('bsr,brf->bsf', jnp.einsum('bsd,bdr->bsr', x, Ai), Bi)
            return base + lora
        key = jax.random.key(seed)
        ks = jax.random.split(key, 10)
        H, I, N, R = (256, 1024, 8, 16)
        B, S = (4, 256)
        std_h = 1.0 / np.sqrt(H)
        std_i = 1.0 / np.sqrt(I)
        x = jax.random.normal(ks[0], (B, S, H), dtype=jnp.float32)
        adapter_indices = jax.random.randint(ks[1], (B,), 0, N, dtype=jnp.int32)
        Wg = jax.random.normal(ks[2], (H, I), dtype=jnp.float32) * std_h
        Wu = jax.random.normal(ks[3], (H, I), dtype=jnp.float32) * std_h
        Wd = jax.random.normal(ks[4], (I, H), dtype=jnp.float32) * std_i
        Ag = jax.random.normal(ks[5], (N, H, R), dtype=jnp.float32) * std_h
        Bg = jnp.zeros((N, R, I), dtype=jnp.float32) + 0.01
        Au = jax.random.normal(ks[6], (N, H, R), dtype=jnp.float32) * std_h
        Bu = jnp.zeros((N, R, I), dtype=jnp.float32) + 0.01
        Ad = jax.random.normal(ks[7], (N, I, R), dtype=jnp.float32) * std_i
        Bd = jnp.zeros((N, R, H), dtype=jnp.float32) + 0.01
        return {'x': x, 'Wg': Wg, 'Wu': Wu, 'Wd': Wd, 'Ag': Ag, 'Bg': Bg, 'Au': Au, 'Bu': Bu, 'Ad': Ad, 'Bd': Bd, 'adapter_indices': adapter_indices}
    _L1_cond_all = _L1_cond_setup()
    _L1_cond_in = {k: v for k, v in _L1_cond_all.items() if k in ('Wg', 'Wu', 'Wd', 'Ag', 'Bg', 'Au', 'Bu', 'Ad', 'Bd')}
    del _L1_cond_all

    def _L1_ffn_setup():
        import jax, jax.numpy as jnp
        import numpy as np
        B, S, H = (2, 256, 256)
        E, K = (16, 4)
        I_MOE, I_SH = (176, 704)
        key = jax.random.key(seed)
        ks = jax.random.split(key, 9)

        def w(k, shape, fan_in):
            return jax.random.normal(k, shape, jnp.float32) * fan_in ** (-0.5)
        return {'hidden_states': jax.random.normal(ks[0], (B, S, H), jnp.float32), 'router_w': w(ks[1], (E, H), H), 'w_gate': w(ks[2], (E, H, I_MOE), H), 'w_up': w(ks[3], (E, H, I_MOE), H), 'w_down': w(ks[4], (E, I_MOE, H), I_MOE), 'sh_gate': w(ks[5], (H, I_SH), H), 'sh_up': w(ks[6], (H, I_SH), H), 'sh_down': w(ks[7], (I_SH, H), I_SH), 'sh_gate_w': w(ks[8], (H, 1), H)}
    _L1_ffn_all = _L1_ffn_setup()
    _L1_ffn_in = {k: v for k, v in _L1_ffn_all.items() if k in ('router_w', 'w_gate', 'w_up', 'w_down', 'sh_gate', 'sh_up', 'sh_down', 'sh_gate_w')}
    del _L1_ffn_all
    return {'x': x, 'itok_B_0_7': itok_B_0_7, 'L0_cond_weights': _L0_cond_in['weights'], 'L0_ffn_Wr': _L0_ffn_in['Wr'], 'L0_ffn_Wg': _L0_ffn_in['Wg'], 'L0_ffn_Wu': _L0_ffn_in['Wu'], 'L0_ffn_Wd': _L0_ffn_in['Wd'], 'L1_cond_Wg': _L1_cond_in['Wg'], 'L1_cond_Wu': _L1_cond_in['Wu'], 'L1_cond_Wd': _L1_cond_in['Wd'], 'L1_cond_Ag': _L1_cond_in['Ag'], 'L1_cond_Bg': _L1_cond_in['Bg'], 'L1_cond_Au': _L1_cond_in['Au'], 'L1_cond_Bu': _L1_cond_in['Bu'], 'L1_cond_Ad': _L1_cond_in['Ad'], 'L1_cond_Bd': _L1_cond_in['Bd'], 'L1_ffn_router_w': _L1_ffn_in['router_w'], 'L1_ffn_w_gate': _L1_ffn_in['w_gate'], 'L1_ffn_w_up': _L1_ffn_in['w_up'], 'L1_ffn_w_down': _L1_ffn_in['w_down'], 'L1_ffn_sh_gate': _L1_ffn_in['sh_gate'], 'L1_ffn_sh_up': _L1_ffn_in['sh_up'], 'L1_ffn_sh_down': _L1_ffn_in['sh_down'], 'L1_ffn_sh_gate_w': _L1_ffn_in['sh_gate_w']}

def reference(x, itok_B_0_7, L0_cond_weights, L0_ffn_Wr, L0_ffn_Wg, L0_ffn_Wu, L0_ffn_Wd, L1_cond_Wg, L1_cond_Wu, L1_cond_Wd, L1_cond_Ag, L1_cond_Bg, L1_cond_Au, L1_cond_Bu, L1_cond_Ad, L1_cond_Bd, L1_ffn_router_w, L1_ffn_w_gate, L1_ffn_w_up, L1_ffn_w_down, L1_ffn_sh_gate, L1_ffn_sh_up, L1_ffn_sh_down, L1_ffn_sh_gate_w):
    import jax
    import jax.numpy as jnp

    def _L0_cond_ref(x, subjects, weights):
        import jax, jax.numpy as jnp
        import numpy as np
        B, C, D, T, N_SUBJECTS = (128, 32, 32, 256, 8)
        w = weights[subjects]
        out = jnp.einsum('bct,bcd->bdt', x, w)
        return out

    def _L0_ffn_ref(x, Wr, Wg, Wu, Wd):
        import jax, jax.numpy as jnp
        import numpy as np
        E = 8
        CAPACITY_FACTOR = 1.25
        B, T, H, I = (4, 128, 256, 176)
        Bb, Tt, Hh = x.shape
        N = Bb * Tt
        cap = max(1, int(CAPACITY_FACTOR * (N * 2 / E)))
        xf = x.reshape(N, Hh)
        logits = jnp.einsum('nh,eh->ne', xf, Wr)
        gate = jax.nn.softmax(logits, axis=-1)
        top2_val, top2_idx = jax.lax.top_k(gate, 2)
        flat_idx = jnp.concatenate([top2_idx[:, 0], top2_idx[:, 1]])
        flat_val = jnp.concatenate([top2_val[:, 0], top2_val[:, 1]])
        onehot = jax.nn.one_hot(flat_idx, E, dtype=jnp.int32)
        rank = (jnp.cumsum(onehot, axis=0) * onehot).sum(-1)
        keep = rank <= cap
        w_assign = jnp.where(keep, flat_val, 0.0)
        tok = jnp.tile(jnp.arange(N), 2)
        comb = jnp.zeros((N, E), x.dtype).at[tok, flat_idx].add(w_assign)
        g = jax.nn.silu(jnp.einsum('nh,eih->eni', xf, Wg))
        u = jnp.einsum('nh,eih->eni', xf, Wu)
        out_e = jnp.einsum('eni,ehi->enh', g * u, Wd)
        y = jnp.einsum('ne,enh->nh', comb, out_e)
        return y.reshape(Bb, Tt, Hh)

    def _L1_cond_ref(x, Wg, Wu, Wd, Ag, Bg, Au, Bu, Ad, Bd, adapter_indices):
        import jax, jax.numpy as jnp
        import numpy as np

        def _lora_linear(x, W, A, B, adapter_indices):
            base = jnp.einsum('bsd,df->bsf', x, W)
            Ai = A[adapter_indices]
            Bi = B[adapter_indices]
            lora = jnp.einsum('bsr,brf->bsf', jnp.einsum('bsd,bdr->bsr', x, Ai), Bi)
            return base + lora
        gate = _lora_linear(x, Wg, Ag, Bg, adapter_indices)
        up = _lora_linear(x, Wu, Au, Bu, adapter_indices)
        h = jax.nn.silu(gate) * up
        return _lora_linear(h, Wd, Ad, Bd, adapter_indices)

    def _L1_ffn_ref(hidden_states, router_w, w_gate, w_up, w_down, sh_gate, sh_up, sh_down, sh_gate_w):
        import jax, jax.numpy as jnp
        import numpy as np
        B, S, H = (2, 256, 256)
        E, K = (16, 4)
        I_MOE, I_SH = (176, 704)
        orig = hidden_states.shape
        h = hidden_states.reshape(-1, orig[-1])
        N = h.shape[0]
        logits = h @ router_w.T
        probs = jax.nn.softmax(logits.astype(jnp.float32), axis=-1)
        top_vals, top_idx = jax.lax.top_k(probs, K)
        top_vals = top_vals / jnp.maximum(top_vals.sum(-1, keepdims=True), 1e-09)
        top_vals = top_vals.astype(h.dtype)
        comb = jnp.zeros((N, E), h.dtype).at[jnp.arange(N)[:, None], top_idx].add(top_vals)
        g = jnp.einsum('nh,ehi->eni', h, w_gate)
        u = jnp.einsum('nh,ehi->eni', h, w_up)
        y = jnp.einsum('eni,eih->enh', jax.nn.silu(g) * u, w_down)
        routed = jnp.einsum('enh,ne->nh', y, comb)
        shared = jax.nn.silu(h @ sh_gate) * (h @ sh_up) @ sh_down
        sg = jax.nn.sigmoid(h @ sh_gate_w)
        return (routed + sg * shared).reshape(orig)
    x = x + _L0_ffn_ref(_L0_cond_ref(x, itok_B_0_7, L0_cond_weights), L0_ffn_Wr, L0_ffn_Wg, L0_ffn_Wu, L0_ffn_Wd)
    x = x + _L1_ffn_ref(_L1_cond_ref(x, L1_cond_Wg, L1_cond_Wu, L1_cond_Wd, L1_cond_Ag, L1_cond_Bg, L1_cond_Au, L1_cond_Bu, L1_cond_Ad, L1_cond_Bd, itok_B_0_7), L1_ffn_router_w, L1_ffn_w_gate, L1_ffn_w_up, L1_ffn_w_down, L1_ffn_sh_gate, L1_ffn_sh_up, L1_ffn_sh_down, L1_ffn_sh_gate_w)
    return x

_drawn_inputs = setup_inputs


def setup_inputs(seed=0):
    import zlib

    import numpy as np

    out = dict(_drawn_inputs(seed))
    spreads = {'L1_cond_Bg': (0.009999999776482582, 0.2),
     'L1_cond_Bu': (0.009999999776482582, 0.2),
     'L1_cond_Bd': (0.009999999776482582, 0.2)}
    factors = {}
    for name, (base, spread) in spreads.items():
        noise = np.random.default_rng([zlib.crc32(name.encode()), seed]).standard_normal(out[name].shape)
        drawn = base * np.exp(spread * noise) if base else spread * noise
        out[name] = jnp.asarray(drawn.astype(out[name].dtype))
    for name, factor in factors.items():
        out[name] = (out[name] * factor).astype(out[name].dtype)
    return out
```

```python
from contextlib import ExitStack

import numpy as np
import concourse.bass as bass
from concourse import mybir

F32 = mybir.dt.float32
F32R = mybir.dt.float32r
BF16 = mybir.dt.bfloat16
I32 = mybir.dt.int32
U32 = mybir.dt.uint32
ALU = mybir.AluOpType
ACT = mybir.ActivationFunctionType
AX_X = mybir.AxisListType.X

P = 128
H = 256
KH = H // P
B, S = 32, 32
N = B * S
NT = N // P
HALF = N // 2
BG = P // S
SUBJ = 8
RANK = 16
I_EXP = 176
GRP = 16
GPE = I_EXP // GRP
E0, K0 = 8, 2
CAP = max(1, int(1.25 * (N * 2 / E0)))
E1, K1 = 16, 4
I_SH = 704
LOGIT1 = E1 + 2
I_COND = 1024
L0, COND, L1 = 0, 1, 2
NC = {L0: E0 * I_EXP // P, COND: I_COND // P, L1: -(-(E1 * I_EXP + I_SH) // P)}
C0 = {L0: 0, COND: NC[L0], L1: NC[L0] + NC[COND]}
KIN = {L0: KH, COND: KH + 1, L1: KH}
MOUT = {L0: KH, COND: KH + 1, L1: KH}
WIDTH = {s: (2 * KIN[s] + MOUT[s]) * P for s in NC}
WMAX = max(WIDTH.values())
PSEUDO = -(-(NC[L1] * P // GRP) // GPE)
SM_R0 = 0
SM_A = SM_R0 + KH * E0
SM_BD = SM_A + KH * 2 * P
SM_R1 = SM_BD + H
SM_N = SM_R1 + KH * LOGIT1
CS_ID, CS_TRI, CS_IOTA, CS_BLK, CS_AD = 0, P, 2 * P, 2 * P + 16, 2 * P + 16 + BG
CS_N = CS_AD + 4


def build(nc, d):
    with ExitStack() as ctx:
        def sb(name, shape, dt=F32):
            return ctx.enter_context(nc.sbuf_tensor(name, shape, dt))

        def sem(name):
            return ctx.enter_context(nc.semaphore(name))

        cst = sb("cst", [P, CS_N])
        idx_i = sb("idx_i", [P, B], I32)
        idx_f = sb("idx_f", [P, B])
        tri = sb("tri", [P, P], BF16)
        ones = sb("ones", [P, P], BF16)
        small = sb("small", [P, SM_N])
        small_hi = sb("small_hi", [P, SM_N], F32R)
        small_lo = sb("small_lo", [P, SM_N], F32R)
        wsub = sb("wsub", [P, SUBJ, S])
        x_tok = sb("x_tok", [P, NT, H])
        x_tok_hi = sb("x_tok_hi", [P, NT, H], F32R)
        x_tok_lo = sb("x_tok_lo", [P, NT, H], F32R)
        xT = sb("xT", [P, KH, N])
        act_hi = sb("act_hi", [P, KH, N], F32R)
        act_lo = sb("act_lo", [P, KH, N], F32R)
        idx_m = sb("idx_m", [P, NT, BG])
        idx_t = sb("idx_t", [P, NT])
        subj_oh = sb("subj_oh", [P, NT, SUBJ])
        wsel8 = sb("wsel8", [P, NT, S, SUBJ])
        wsel = sb("wsel", [P, NT, S])
        wblk = sb("wblk", [P, NT, BG, S])
        wblk_hi = sb("wblk_hi", [P, N], F32R)
        wblk_lo = sb("wblk_lo", [P, N], F32R)
        lmask = sb("lmask", [P, B])
        r_max = sb("r_max", [P, NT])
        r_lg = sb("r_lg", [P, NT, E1])
        r_ex = sb("r_ex", [P, NT, E1])
        r_sum = sb("r_sum", [P, NT])
        r_rec = sb("r_rec", [P, NT])
        r_gate = sb("r_gate", [P, NT, E1])
        r_top = sb("r_top", [P, NT, 8])
        r_idx = sb("r_idx", [P, NT, 8], U32)
        r_idf = sb("r_idf", [P, NT, 8])
        r_oh = sb("r_oh", [P, K1, NT, E1])
        r_ohb = sb("r_ohb", [P, K0, NT, E0], BF16)
        r_kept = sb("r_kept", [P, K1, NT, E1])
        comb = sb("comb", [P, NT, PSEUDO])
        combT = sb("combT", [PSEUDO, N])
        w_raw = [sb(f"w_raw{i}", [P, WMAX]) for i in range(2)]
        w_hi = [sb(f"w_hi{i}", [P, WMAX], F32R) for i in range(2)]
        w_lo = [sb(f"w_lo{i}", [P, WMAX], F32R) for i in range(2)]
        comb_b = [sb(f"comb_b{i}", [P, N]) for i in range(2)]
        silu = [sb(f"silu{i}", [P, HALF]) for i in range(2)]
        prod = [sb(f"prod{i}", [P, HALF]) for i in range(2)]
        hid = [sb(f"hid{i}", [P, HALF]) for i in range(2)]
        hid_hi = [sb(f"hid_hi{i}", [P, HALF], F32R) for i in range(2)]
        hid_lo = [sb(f"hid_lo{i}", [P, HALF], F32R) for i in range(2)]
        la = sb("la", [P, 2, N])
        la_hi = sb("la_hi", [P, 2, N], F32R)
        la_lo = sb("la_lo", [P, 2, N], F32R)

        def bank(name):
            return ctx.enter_context(nc.psum_tensor(name, [P, 512], F32))
        Y = [[bank(f"y{m}{s}") for s in range(2)] for m in range(KH)]
        GU = [[bank(f"gu{s}{j}") for j in range(2)] for s in range(2)]
        HA = GU[1]
        logit_ps, rank_ps = Y[0][0], Y[0][1]
        combT_ps = Y[1]

        s_in = {k: sem("in_" + k) for k in ("cst", "idx", "small", "wsub", "xtok", "xT")}
        s_raw = [sem(f"raw_landed{i}") for i in range(2)]
        s_comb = [sem(f"comb_landed{i}") for i in range(2)]
        s_scr = sem("scratch_written")
        s_out = sem("out_written")
        s_whi = sem("w_hi_ready")
        s_w = sem("w_split")
        s_small = sem("small_split")
        s_g, s_u, s_d = sem("gate_done"), sem("up_done"), sem("down_done")
        s_silu, s_prod, s_h = sem("silu_done"), sem("prod_done"), sem("hid_done")
        s_hh, s_hl = sem("hid_hi_done"), sem("hid_lo_done")
        s_chain = sem("dve_chain")
        s_blk, s_blkh, s_blkl = sem("wblk_ready"), sem("wblk_hi_ready"), sem("wblk_lo_ready")
        s_xth, s_xtl = sem("xtok_hi_ready"), sem("xtok_lo_ready")
        s_xc = sem("cond0_done")
        s_act, s_acth, s_actl = sem("act_ready"), sem("act_hi_ready"), sem("act_lo_ready")
        s_cb16 = sem("bf16_consts")
        s_logit, s_rlg, s_exp = sem("logits_done"), sem("shifted_ready"), sem("exp_done")
        s_oh, s_rank = sem("onehot_ready"), sem("rank_done")
        s_cmb, s_cmbT, s_cmbS = sem("comb_ready"), sem("combT_done"), sem("combT_in_sbuf")
        s_la, s_lam, s_lah, s_lal = sem("lora_done"), sem("lora_masked"), sem("lora_hi"), sem("lora_lo")
        s_bd = sem("lora_down_done")
        s_sig = sem("sig_exp_done")
        s_res = sem("residual_out")

        block = ctx.enter_context(nc.Block())

        def half(s):
            return slice(s * HALF, (s + 1) * HALF)

        def moe_unit(st, n):
            return n if st == L0 else n - 2 * NC[COND]

        def run_chunks(eng, st, chunk):
            chunk(C0[st], C0[st] % 2, 0)
            pairs = (NC[st] - 2) // 2
            with eng.Fori(0, pairs) as i:
                for k in range(2):
                    chunk(C0[st] + 1 + k + 2 * i, (C0[st] + 1 + k) % 2, 1)
            for c in range(1 + 2 * pairs, NC[st]):
                chunk(C0[st] + c, (C0[st] + c) % 2, 2 if c == NC[st] - 1 else 1)

        def wait_pos(eng, s, v):
            if not isinstance(v, int) or v > 0:
                eng.wait_ge(s, v)

        @block.sync
        def _(sp):
            sp.dma_start(cst[:], d["cst"]).then_inc(s_in["cst"], 16)
            sp.dma_start(idx_i[:], d["idx"].broadcast_to([P, B])).then_inc(s_in["idx"], 16)
            sp.dma_start(wsub[:], d["wsub"]).then_inc(s_in["wsub"], 16)
            sp.dma_start(x_tok[:], d["x_tok"]).then_inc(s_in["xtok"], 16)
            sp.dma_start(small[:], d["small"]).then_inc(s_in["small"], 16)

            def raw(st, c, par):
                wait_pos(sp, s_w, c - 1)
                sp.dma_start(w_raw[par][:, 0:WIDTH[st]], d["w"][st][bass.ds(c - C0[st], 1)]
                             .rearrange("a p n -> (a p) n")).then_inc(s_raw[par], 16)

            def combs(st, c, par):
                wait_pos(sp, s_h, moe_unit(st, 2 * c - 2))
                for g in range(P // GRP):
                    sp.dma_start(comb_b[par][g * GRP:(g + 1) * GRP, :],
                                 d["scr"][st][bass.ds((c - C0[st]) * (P // GRP) + g, 1)]
                                 .broadcast_to([GRP, N])).then_inc(s_comb[par], 16)

            for st in (L0, COND, L1):
                for c in range(2):
                    raw(st, C0[st] + c, (C0[st] + c) % 2)
                if st == L0:
                    sp.dma_start(xT[:], d["xT"]).then_inc(s_in["xT"], 16)
                if st == COND:
                    with sp.Fori(0, (NC[st] - 2) // 2) as i:
                        for k in range(2):
                            raw(st, C0[st] + 2 + k + 2 * i, (C0[st] + k) % 2)
                    continue
                ne = {L0: E0, L1: PSEUDO}[st]
                j = {L0: 1, L1: 2}[st]
                sp.wait_ge(s_cmbS, j)
                for g in range(GPE):
                    sp.dma_start(d["scr"][st].rearrange("(e g) n -> e g n", g=GPE)[:, g, :],
                                 combT[0:ne, :]).then_inc(s_scr, 16)
                sp.wait_ge(s_scr, 16 * GPE * j)

                def chunk(c, par, more):
                    combs(st, c, par)
                    if more:
                        raw(st, c + 2, par)
                chunk(C0[st], C0[st] % 2, True)
                pairs = (NC[st] - 3) // 2
                with sp.Fori(0, pairs) as i:
                    for k in range(2):
                        chunk(C0[st] + 1 + k + 2 * i, (C0[st] + 1 + k) % 2, True)
                for c in range(1 + 2 * pairs, NC[st]):
                    chunk(C0[st] + c, (C0[st] + c) % 2, c + 2 < NC[st])
            for m in range(KH):
                for s in range(2):
                    sp.wait_ge(s_res, m * 2 + s + 1)
                    sp.dma_start(d["out"][:, m, half(s)], xT[:, m, half(s)]).then_inc(s_out, 16)
            sp.wait_ge(s_out, 16 * KH * 2)

        @block.gpsimd
        def _(pool):
            pool.wait_ge(s_in["small"], 16)
            nc.gpsimd.tensor_copy(small_hi[:], small[:]).then_inc(s_small, 1)
            pool.wait_ge(s_small, 1)
            nc.gpsimd.tensor_tensor(small_lo[:], small[:], small_hi[:].bitcast(F32), ALU.subtract).then_inc(s_small, 1)
            for st in (L0, COND, L1):
                def chunk(c, par, where):
                    pool.wait_ge(s_whi, c + 1)
                    w = WIDTH[st]
                    nc.gpsimd.tensor_tensor(w_lo[par][:, 0:w], w_raw[par][:, 0:w], w_hi[par][:, 0:w].bitcast(F32),
                                            ALU.subtract).then_inc(s_w, 1)
                run_chunks(pool, st, chunk)

        @block.scalar
        def _(act):
            def round_weights(st, c, par):
                act.wait_ge(s_raw[par], 8 * (c - par) + 16)
                wait_pos(act, s_d, 2 * c - 2)
                w = WIDTH[st]
                nc.scalar.activation(w_hi[par][:, 0:w], w_raw[par][:, 0:w], ACT.Copy).then_inc(s_whi, 1)

            act.wait_ge(s_in["xtok"], 16)
            nc.scalar.activation(x_tok_hi[:], x_tok[:], ACT.Copy).then_inc(s_xth, 1)
            act.wait_ge(s_blk, 1)
            nc.scalar.activation(wblk_hi[:], wblk[:].rearrange("p t b d -> p (t b d)"), ACT.Copy).then_inc(s_blkh, 1)
            act.wait_ge(s_xc, 1)
            for m in range(KH):
                for s in range(2):
                    nc.scalar.activation(act_hi[:, m, half(s)], Y[m][s][:], ACT.Copy).then_inc(s_acth, 1)

            def route_exp(j, e):
                act.wait_ge(s_rlg, j)
                nc.scalar.activation(r_ex[:, :, 0:e], r_lg[:, :, 0:e], ACT.Exp).then_inc(s_exp, 1)

            def units(st):
                def chunk(c, par, where):
                    for s in range(2):
                        n = 2 * c + s
                        act.wait_ge(s_g, n + 1)
                        wait_pos(act, s_prod, n - 1)
                        gate = GU[0 if st == COND else s][0]
                        nc.scalar.activation(silu[s][:], gate[:], ACT.Silu).then_inc(s_silu, 1)
                        if st == COND:
                            act.wait_ge(s_prod, n + 1)
                        else:
                            act.wait_ge(s_h, moe_unit(st, n) + 1)
                        wait_pos(act, s_d, n - 1)
                        nc.scalar.activation(hid_hi[s][:], hid[s][:], ACT.Copy).then_inc(s_hh, 1)
                        if s == 0 and not (st == L1 and where == 2):
                            round_weights(st + 1 if where == 2 else st, c + 1, 1 - par)
                run_chunks(act, st, chunk)

            round_weights(L0, 0, 0)
            route_exp(1, E0)
            units(L0)
            for m in range(KH):
                for s in range(2):
                    act.wait_ge(s_act, m * 2 + s + 1)
                    nc.scalar.activation(act_hi[:, m, half(s)], xT[:, m, half(s)], ACT.Copy).then_inc(s_acth, 1)
            for s in range(2):
                for j in range(2):
                    act.wait_ge(s_lam, 2 * s + j + 1)
                    nc.scalar.activation(la_hi[:, j, half(s)], la[:, j, half(s)], ACT.Copy).then_inc(s_lah, 1)
            units(COND)
            for s in range(2):
                act.wait_ge(s_lam, 4 + s + 1)
                nc.scalar.activation(la_hi[:, 0, half(s)], la[:, 0, half(s)], ACT.Copy).then_inc(s_lah, 1)
            act.wait_ge(s_bd, 1)
            for m in range(KH):
                for s in range(2):
                    nc.scalar.activation(act_hi[:, m, half(s)], Y[m][s][:], ACT.Copy).then_inc(s_acth, 1)
            route_exp(2, E1)
            nc.scalar.activation(r_max[:], logit_ps[:, 0:NT * LOGIT1].rearrange("p (t e) -> p t e", t=NT)[:, :, E1],
                                 ACT.Exp, scale=-1.0).then_inc(s_sig, 1)
            units(L1)

        @block.vector
        def _(dve):
            count = [0]

            def chain(ins):
                count[0] += 1
                ins.then_inc(s_chain, 1)
                dve.wait_ge(s_chain, count[0])

            V = nc.vector
            blkm = cst[:, CS_BLK:CS_BLK + BG]
            dve.wait_ge(s_in["cst"], 16)
            dve.wait_ge(s_in["idx"], 16)
            chain(V.tensor_copy(idx_f[:], idx_i[:]))
            chain(V.tensor_tensor(idx_m[:], idx_f[:].rearrange("p (t b) -> p t b", b=BG),
                                  blkm.unsqueeze(1).broadcast_to([P, NT, BG]), ALU.mult))
            chain(V.reduce_sum(idx_t[:], idx_m[:], axis=AX_X))
            chain(V.tensor_tensor(subj_oh[:], cst[:, CS_IOTA:CS_IOTA + SUBJ].unsqueeze(1).broadcast_to([P, NT, SUBJ]),
                                  idx_t[:].unsqueeze(2).broadcast_to([P, NT, SUBJ]), ALU.is_equal))
            dve.wait_ge(s_in["wsub"], 16)
            chain(V.tensor_tensor(wsel8[:],
                                  wsub[:].rearrange("p s d -> p d s").unsqueeze(1).broadcast_to([P, NT, S, SUBJ]),
                                  subj_oh[:].unsqueeze(2).broadcast_to([P, NT, S, SUBJ]), ALU.mult))
            chain(V.reduce_sum(wsel[:], wsel8[:], axis=AX_X))
            V.tensor_tensor(wblk[:], wsel[:].unsqueeze(2).broadcast_to([P, NT, BG, S]),
                            blkm.unsqueeze(1).unsqueeze(3).broadcast_to([P, NT, BG, S]),
                            ALU.mult).then_inc(s_blk, 1)
            V.tensor_scalar(lmask[:], idx_f[:], cst[:, CS_AD:CS_AD + 1], None, ALU.is_equal).then_inc(s_cb16, 1)
            V.tensor_copy(tri[:], cst[:, CS_TRI:CS_TRI + P]).then_inc(s_cb16, 1)
            V.memset(ones[:], 1.0).then_inc(s_cb16, 1)
            dve.wait_ge(s_xth, 1)
            V.tensor_tensor(x_tok_lo[:], x_tok[:], x_tok_hi[:].bitcast(F32), ALU.subtract).then_inc(s_xtl, 1)
            dve.wait_ge(s_blkh, 1)
            V.tensor_tensor(wblk_lo[:], wblk[:].rearrange("p t b d -> p (t b d)"), wblk_hi[:].bitcast(F32),
                            ALU.subtract).then_inc(s_blkl, 1)

            def split_y(base):
                for m in range(KH):
                    for s in range(2):
                        dve.wait_ge(s_acth, base + m * 2 + s + 1)
                        V.tensor_tensor(act_lo[:, m, half(s)], Y[m][s][:], act_hi[:, m, half(s)].bitcast(F32),
                                        ALU.subtract).then_inc(s_actl, 1)

            def top(lg, ne, j):
                chain(V.reduce_max(r_sum[:], lg, axis=AX_X))
                V.tensor_tensor(r_lg[:, :, 0:ne], lg, r_sum[:].unsqueeze(2).broadcast_to([P, NT, ne]),
                                ALU.subtract).then_inc(s_rlg, 1)
                dve.wait_ge(s_exp, j)
                chain(V.reduce_sum(r_sum[:], r_ex[:, :, 0:ne], axis=AX_X))
                chain(V.reciprocal(r_rec[:], r_sum[:]))
                chain(V.tensor_tensor(r_gate[:, :, 0:ne], r_ex[:, :, 0:ne],
                                      r_rec[:].unsqueeze(2).broadcast_to([P, NT, ne]), ALU.mult))
                for t in range(NT - 1):
                    V.max(r_top[:, t, :], r_gate[:, t, 0:ne])
                chain(V.max(r_top[:, NT - 1, :], r_gate[:, NT - 1, 0:ne]))
                for t in range(NT - 1):
                    V.max_index(r_idx[:, t, :], r_top[:, t, :], r_gate[:, t, 0:ne])
                chain(V.max_index(r_idx[:, NT - 1, :], r_top[:, NT - 1, :], r_gate[:, NT - 1, 0:ne]))
                chain(V.tensor_copy(r_idf[:], r_idx[:]))

            def onehot(out, ne, k):
                iota = cst[:, CS_IOTA:CS_IOTA + ne].unsqueeze(1).broadcast_to([P, NT, ne])
                return V.tensor_tensor(out[:, k, :, 0:ne], iota,
                                       r_idf[:, :, k].unsqueeze(2).broadcast_to([P, NT, ne]), ALU.is_equal)

            def comb_out(j, ne):
                for s in range(2):
                    dve.wait_ge(s_cmbT, 2 * j + s - 1)
                    ins = V.tensor_copy(combT[0:ne, half(s)], combT_ps[s][0:ne, :])
                ins.then_inc(s_cmbS, 1)

            def units(st):
                def chunk(c, par, where):
                    for s in range(2):
                        n = 2 * c + s
                        dve.wait_ge(s_u, n + 1)
                        dve.wait_ge(s_silu, n + 1)
                        up = GU[0 if st == COND else s][1]
                        out = hid[s] if st == COND else prod[s]
                        V.tensor_tensor(out[:], silu[s][:], up[:], ALU.mult).then_inc(s_prod, 1)
                        if st != COND:
                            dve.wait_ge(s_prod, n + 1)
                            if s == 0:
                                k = c if st == L0 else c - NC[COND]
                                kp = par if st == L0 else (par + NC[COND]) % 2
                                dve.wait_ge(s_comb[par], (k - kp) * 64 + 128)
                            V.tensor_tensor(hid[s][:], prod[s][:], comb_b[par][:, half(s)],
                                            ALU.mult).then_inc(s_h, 1)
                        dve.wait_ge(s_hh, n + 1)
                        wait_pos(dve, s_d, n - 1)
                        V.tensor_tensor(hid_lo[s][:], hid[s][:], hid_hi[s][:].bitcast(F32),
                                        ALU.subtract).then_inc(s_hl, 1)
                run_chunks(dve, st, chunk)

            dve.wait_ge(s_xc, 1)
            split_y(0)
            dve.wait_ge(s_logit, 1)
            top(logit_ps[:, 0:NT * E0].rearrange("p (t e) -> p t e", t=NT), E0, 1)
            onehot(r_ohb, E0, 0)
            onehot(r_ohb, E0, 1).then_inc(s_oh, 1)
            dve.wait_ge(s_oh, 1)
            dve.wait_ge(s_rank, 1)
            rank = rank_ps[:, 0:K0 * NT * E0].rearrange("p (k t e) -> p k t e", k=K0, t=NT)
            for k in range(K0):
                ins = V.scalar_tensor_tensor(out=r_kept[:, k, :, 0:E0], in0=rank[:, k], scalar=float(CAP),
                                             in1=r_ohb[:, k], op0=ALU.is_le, op1=ALU.mult)
            chain(ins)
            for k in range(K0):
                ins = V.tensor_tensor(r_oh[:, k, :, 0:E0], r_kept[:, k, :, 0:E0],
                                      r_top[:, :, k].unsqueeze(2).broadcast_to([P, NT, E0]), ALU.mult)
            chain(ins)
            V.tensor_tensor(comb[:, :, 0:E0], r_oh[:, 0, :, 0:E0], r_oh[:, 1, :, 0:E0], ALU.add).then_inc(s_cmb, 1)
            comb_out(1, E0)
            units(L0)

            dve.wait_ge(s_in["xT"], 16)
            dve.wait_ge(s_d, 2 * C0[COND])
            for m in range(KH):
                for s in range(2):
                    V.tensor_tensor(xT[:, m, half(s)], xT[:, m, half(s)], Y[m][s][:], ALU.add).then_inc(s_act, 1)
            for m in range(KH):
                for s in range(2):
                    dve.wait_ge(s_acth, 4 + m * 2 + s + 1)
                    V.tensor_tensor(act_lo[:, m, half(s)], xT[:, m, half(s)], act_hi[:, m, half(s)].bitcast(F32),
                                    ALU.subtract).then_inc(s_actl, 1)

            dve.wait_ge(s_cb16, 3)

            def keep_adapter(j, s, ps, k):
                mask = lmask[:, s * B // 2:(s + 1) * B // 2].unsqueeze(2).broadcast_to([P, B // 2, S])
                V.tensor_tensor(la[:, j, half(s)].rearrange("p (b t) -> p b t", t=S),
                                ps[:].rearrange("p (b t) -> p b t", t=S), mask, ALU.mult).then_inc(s_lam, 1)
                dve.wait_ge(s_lah, k)
                V.tensor_tensor(la_lo[:, j, half(s)], la[:, j, half(s)], la_hi[:, j, half(s)].bitcast(F32),
                                ALU.subtract).then_inc(s_lal, 1)

            for s in range(2):
                for j in range(2):
                    dve.wait_ge(s_la, 2 * s + j + 1)
                    keep_adapter(j, s, GU[s][j], 2 * s + j + 1)
            units(COND)
            dve.wait_ge(s_d, 2 * C0[L1])
            for s in range(2):
                keep_adapter(0, s, HA[s], 4 + s + 1)

            split_y(8)
            dve.wait_ge(s_logit, 2)
            top(logit_ps[:, 0:NT * LOGIT1].rearrange("p (t e) -> p t e", t=NT)[:, :, 0:E1], E1, 2)
            for k in range(K1):
                onehot(r_oh, E1, k)
            chain(V.reduce_sum(r_sum[:], r_top[:, :, 0:K1], axis=AX_X))
            dve.wait_ge(s_sig, 1)
            chain(V.tensor_scalar(r_sum[:], r_sum[:], 1e-9, None, ALU.max))
            chain(V.reciprocal(r_rec[:], r_sum[:]))
            chain(V.tensor_tensor(r_top[:, :, 0:K1], r_top[:, :, 0:K1],
                                  r_rec[:].unsqueeze(2).broadcast_to([P, NT, K1]), ALU.mult))
            for k in range(K1):
                ins = V.tensor_tensor(r_kept[:, k], r_oh[:, k],
                                      r_top[:, :, k].unsqueeze(2).broadcast_to([P, NT, E1]), ALU.mult)
            chain(ins)
            V.tensor_tensor(r_oh[:, 0], r_kept[:, 0], r_kept[:, 1], ALU.add)
            chain(V.tensor_tensor(r_oh[:, 1], r_kept[:, 2], r_kept[:, 3], ALU.add))
            V.tensor_tensor(comb[:, :, 0:E1], r_oh[:, 0], r_oh[:, 1], ALU.add)
            chain(V.tensor_scalar(r_max[:], r_max[:], 1.0, None, ALU.add))
            chain(V.reciprocal(r_rec[:], r_max[:]))
            V.tensor_copy(comb[:, :, E1:PSEUDO], r_rec[:].unsqueeze(2).broadcast_to([P, NT, PSEUDO - E1])
                          ).then_inc(s_cmb, 1)
            comb_out(2, PSEUDO)
            units(L1)
            dve.wait_ge(s_d, 2 * (C0[L1] + NC[L1]))
            for m in range(KH):
                for s in range(2):
                    V.tensor_tensor(xT[:, m, half(s)], xT[:, m, half(s)], Y[m][s][:], ALU.add).then_inc(s_res, 1)

        @block.tensor
        def _(pe):
            T = nc.tensor

            def mm3(out, w, x, start, stop):
                T.matmul(out, w[0], x[0], start=start, stop=False)
                T.matmul(out, w[0], x[1], start=False, stop=False)
                return T.matmul(out, w[1], x[0], start=False, stop=stop)

            def parts(t, *ix):
                return tuple(a[ix] for a in t)

            ACTV, SMALL, LA = (act_hi, act_lo), (small_hi, small_lo), (la_hi, la_lo)
            A = slice(None)

            for s in (s_xth, s_xtl, s_blkh, s_blkl):
                pe.wait_ge(s, 1)
            for t in range(NT):
                for m in range(KH):
                    last = mm3(Y[m][t // 4][:, (t % 4) * P:(t % 4 + 1) * P],
                               parts((x_tok_hi, x_tok_lo), A, t, slice(m * P, (m + 1) * P)),
                               parts((wblk_hi, wblk_lo), A, slice(t * P, (t + 1) * P)), True, True)
            last.then_inc(s_xc, 1)

            def logits(lo_done, off, ne):
                pe.wait_ge(s_small, 2)
                pe.wait_ge(s_actl, lo_done)
                for t in range(NT):
                    for k in range(KH):
                        last = mm3(logit_ps[:, t * ne:(t + 1) * ne], parts(ACTV, A, k, slice(t * P, (t + 1) * P)),
                                   parts(SMALL, A, slice(off + k * ne, off + (k + 1) * ne)), k == 0, k == KH - 1)
                last.then_inc(s_logit, 1)

            def comb_transposed(j, ne):
                pe.wait_ge(s_cmb, j)
                for t in range(NT):
                    ins = T.transpose(combT_ps[t // 4][0:ne, (t % 4) * P:(t % 4 + 1) * P], comb[:, t, 0:ne],
                                      cst[:, CS_ID:CS_ID + P])
                    if t % 4 == 3:
                        ins.then_inc(s_cmbT, 1)

            def units(st, hook):
                K, M = KIN[st], MOUT[st]

                def gate_up(c, par, s):
                    n = 2 * c + s
                    back = 1 if st == COND else 2
                    wait_pos(pe, s_silu, n + 1 - back)
                    wait_pos(pe, s_prod, n + 1 - back)
                    for j, done in ((0, s_g), (1, s_u)):
                        for k in range(K):
                            x = parts(ACTV, A, k, half(s)) if k < KH else parts(LA, A, j, half(s))
                            last = mm3(GU[0 if st == COND else s][j][:],
                                       parts((w_hi[par], w_lo[par]), A, slice((j * K + k) * P, (j * K + k + 1) * P)),
                                       x, k == 0, k == K - 1)
                        last.then_inc(done, 1)

                def down(c, par, s, start, stop):
                    n = 2 * c + s
                    pe.wait_ge(s_hh, n + 1)
                    pe.wait_ge(s_hl, n + 1)
                    for m in range(M):
                        out = Y[m][s] if m < KH else HA[s]
                        closed = stop and (st != COND or m == KH)
                        off = (2 * K + m) * P
                        last = mm3(out[:], parts((w_hi[par], w_lo[par]), A, slice(off, off + P)),
                                   (hid_hi[s][:], hid_lo[s][:]), start, closed)
                    last.then_inc(s_d, 1)

                def first_chunk():
                    c, par = C0[st], C0[st] % 2
                    pe.wait_ge(s_w, c + 1)
                    gate_up(c, par, 0)
                    hook[0]()
                    gate_up(c, par, 1)
                    hook[1]()
                    down(c, par, 0, True, False)
                    down(c, par, 1, True, False)
                    c, par = c + 1, 1 - par
                    pe.wait_ge(s_w, c + 1)
                    gate_up(c, par, 0)
                    gate_up(c, par, 1)
                    down(c, par, 0, False, False)

                def mid(c, par):
                    pe.wait_ge(s_w, c + 1)
                    gate_up(c, par, 0)
                    down(c - 1, 1 - par, 1, False, False)
                    gate_up(c, par, 1)
                    down(c, par, 0, False, False)

                first_chunk()
                pairs = (NC[st] - 3) // 2
                with pe.Fori(0, pairs) as i:
                    for k in range(2):
                        mid(C0[st] + 2 + k + 2 * i, (C0[st] + k) % 2)
                for c in range(2 + 2 * pairs, NC[st] - 1):
                    mid(C0[st] + c, (C0[st] + c) % 2)
                c = C0[st] + NC[st] - 1
                par = c % 2
                pe.wait_ge(s_w, c + 1)
                gate_up(c, par, 0)
                down(c - 1, 1 - par, 1, False, False)
                gate_up(c, par, 1)
                down(c, par, 0, False, True)
                down(c, par, 1, False, True)

            def ranks():
                pe.wait_ge(s_cb16, 3)
                pe.wait_ge(s_oh, 1)
                oh = r_ohb[:].rearrange("p k t e -> p (k t e)")
                total = K0 * NT * E0
                T.matmul(rank_ps[:, 0:total], tri[:], oh, start=True, stop=False)
                for b in range(1, K0 * NT):
                    last = T.matmul(rank_ps[:, b * E0:total], ones[:], oh[:, 0:total - b * E0], start=False,
                                    stop=b == K0 * NT - 1)
                last.then_inc(s_rank, 1)

            logits(4, SM_R0, E0)
            units(L0, (ranks, lambda: comb_transposed(1, E0)))

            pe.wait_ge(s_actl, 8)
            for s in range(2):
                for j in range(2):
                    for k in range(KH):
                        off = SM_A + (k * 2 + j) * P
                        last = mm3(GU[s][j][:], parts(SMALL, A, slice(off, off + P)), parts(ACTV, A, k, half(s)),
                                   k == 0, k == KH - 1)
                    last.then_inc(s_la, 1)
            pe.wait_ge(s_lal, 4)
            units(COND, (lambda: None, lambda: None))
            for s in range(2):
                pe.wait_ge(s_lah, 4 + s + 1)
                pe.wait_ge(s_lal, 4 + s + 1)
                for m in range(KH):
                    off = SM_BD + m * P
                    last = mm3(Y[m][s][:], parts(SMALL, A, slice(off, off + P)), parts(LA, A, 0, half(s)), False, True)
            last.then_inc(s_bd, 1)

            logits(12, SM_R1, LOGIT1)
            units(L1, (lambda: None, lambda: comb_transposed(2, PSEUDO)))


def chunks(gate, up, down):
    k, i = gate.shape
    n = i // P

    def cols(w):
        return w.reshape(k // P, P, n, P).transpose(2, 1, 0, 3).reshape(n, P, k)
    return np.ascontiguousarray(np.concatenate([cols(gate), cols(up), down.reshape(n, P, -1)], axis=2))


def on_partitions(w):
    return w.reshape(KH, P, -1).transpose(1, 0, 2)


def kernel(**inputs):
    import concourse.bacc as bacc
    from concourse.bass_utils import run_bass_kernel_spmd as run

    a = {k: np.asarray(v) for k, v in inputs.items()}
    x = a["x"].reshape(N, H)
    flat = lambda w: w.transpose(1, 0, 2).reshape(w.shape[1], -1)
    w0 = chunks(a["L0_ffn_Wg"].reshape(-1, H).T, a["L0_ffn_Wu"].reshape(-1, H).T,
                a["L0_ffn_Wd"].transpose(0, 2, 1).reshape(-1, H))
    lo_b = lambda w: w.reshape(SUBJ * RANK, -1)
    wc = chunks(np.concatenate([a["L1_cond_Wg"], lo_b(a["L1_cond_Bg"])]),
                np.concatenate([a["L1_cond_Wu"], lo_b(a["L1_cond_Bu"])]),
                np.concatenate([a["L1_cond_Wd"], flat(a["L1_cond_Ad"])], axis=1))
    pad = NC[L1] * P - E1 * I_EXP - I_SH
    side = lambda w, sh: np.concatenate([flat(w), sh, np.zeros((H, pad), np.float32)], axis=1)
    w1 = chunks(side(a["L1_ffn_w_gate"], a["L1_ffn_sh_gate"]), side(a["L1_ffn_w_up"], a["L1_ffn_sh_up"]),
                np.concatenate([a["L1_ffn_w_down"].reshape(-1, H), a["L1_ffn_sh_down"],
                                np.zeros((pad, H), np.float32)]))
    la = np.stack([on_partitions(flat(a["L1_cond_Ag"])), on_partitions(flat(a["L1_cond_Au"]))], axis=2)
    small = np.concatenate([
        on_partitions(a["L0_ffn_Wr"].T).reshape(P, -1), la.reshape(P, -1), lo_b(a["L1_cond_Bd"]),
        on_partitions(np.concatenate([a["L1_ffn_router_w"].T, a["L1_ffn_sh_gate_w"], np.zeros((H, 1), np.float32)],
                                     axis=1)).reshape(P, -1)], axis=1)
    cst = np.zeros((P, CS_N), np.float32)
    cst[:, CS_ID:CS_ID + P] = np.eye(P)
    cst[:, CS_TRI:CS_TRI + P] = np.triu(np.ones((P, P)))
    cst[:, CS_IOTA:CS_IOTA + 16] = np.arange(16)
    cst[np.arange(P), CS_BLK + np.arange(P) // S] = 1
    cst[:, CS_AD] = np.arange(P) // RANK
    arrays = {
        "cst": cst, "idx": a["itok_B_0_7"].reshape(1, B), "small": small,
        "wsub": np.tile(a["L0_cond_weights"].transpose(1, 0, 2), (BG, 1, 1)),
        "x_tok": x.reshape(NT, P, H).transpose(1, 0, 2), "xT": on_partitions(x.T), "w0": w0, "wc": wc, "w1": w1,
    }
    arrays = {k: np.ascontiguousarray(v) for k, v in arrays.items()}
    nc = bacc.Bacc("TRN2", target_bir_lowering=False, num_devices=1)
    d = {k: nc.dram_tensor("in_" + k, v.shape, mybir.dt.from_np(v.dtype), kind="ExternalInput").ap()
         for k, v in arrays.items()}
    d["w"] = {L0: d["w0"], COND: d["wc"], L1: d["w1"]}
    d["scr"] = {L0: nc.dram_tensor("scr0", (E0 * GPE, N), F32, kind="Internal").ap(),
                L1: nc.dram_tensor("scr1", (PSEUDO * GPE, N), F32, kind="Internal").ap()}
    d["out"] = nc.dram_tensor("out", (P, KH, N), F32, kind="ExternalOutput").ap()
    build(nc, d)
    r = run(nc, [{"in_" + k: v for k, v in arrays.items()}], core_ids=[0])
    out = r.results[0]["out"]
    return np.ascontiguousarray(out.transpose(1, 0, 2).reshape(H, N).T).reshape(B, S, H)
```

```python
from contextlib import ExitStack

import numpy as np
import concourse.bass as bass
from concourse import mybir

F32 = mybir.dt.float32
F32R = mybir.dt.float32r
BF16 = mybir.dt.bfloat16
I32 = mybir.dt.int32
U32 = mybir.dt.uint32
ALU = mybir.AluOpType
ACT = mybir.ActivationFunctionType
AX_X = mybir.AxisListType.X

P = 128
H = 256
KH = H // P
B, S = 32, 32
N = B * S
NT = N // P
HALF = N // 2
BG = P // S
SUBJ = 8
RANK = 16
I_EXP = 176
GRP = 16
GPE = I_EXP // GRP
E0, K0 = 8, 2
CAP = max(1, int(1.25 * (N * 2 / E0)))
E1, K1 = 16, 4
I_SH = 704
LOGIT1 = E1 + 2
I_COND = 1024
L0, COND, SH = 0, 1, 2
STAGES = (L0, COND, SH)
NC = {L0: E0 * I_EXP // P, COND: I_COND // P, SH: -(-I_SH // P)}
C0 = {st: sum(NC[o] for o in STAGES if o < st) for st in STAGES}
SLOT_TILES = N * K1 // P + E1 - 1
RING = 4
AHEAD = RING + 2
HALF_I = I_EXP // 2
GU_N = 2 * I_EXP
ROUTE_N = 2 * SLOT_TILES
KIN = {st: KH + (st == COND) for st in STAGES}
MOUT = {st: KH + (st == COND) for st in STAGES}
WIDTH = {st: (2 * KIN[st] + MOUT[st]) * P for st in STAGES}
WMAX = max(WIDTH.values())
SH_TAIL = I_SH - (NC[SH] - 1) * P
assert 2 * SH_TAIL == P
SM_A = 0
SM_BD = SM_A + KH * 2 * P
SM_SPLIT = SM_BD + H
SM_R0 = 0
SM_R1 = SM_R0 + KH * E0
R_N = SM_R1 + KH * LOGIT1
CS_ID, CS_TRI, CS_N = 0, P, 2 * P
CI_IOTA, CI_BLK, CI_AD = 0, E1, E1 + BG
CI_N = CI_AD + 4
CT_LT, CT_THR = 0, E1 * E1
CT_ROW = CT_THR + NT
CT_TILE = CT_ROW + P
CT_TOK = CT_TILE + SLOT_TILES
CT_N = CT_TOK + NT
W1_PIECES = NC[COND]
W1_EXP = E1 // W1_PIECES
WD_PIECES = NC[SH] - 2
WD_EXP = E1 // WD_PIECES


def build(nc, d):
    with ExitStack() as ctx:
        def sb(name, shape, dt=F32):
            return ctx.enter_context(nc.sbuf_tensor(name, shape, dt))

        def sem(name):
            return ctx.enter_context(nc.semaphore(name))

        cst = sb("cst", [P, CS_N])
        cst0 = sb("cst0", [P, CI_N])
        idx_i = sb("idx_i", [P, B], I32)
        idx_f = sb("idx_f", [P, B])
        tri = sb("tri", [P, P], BF16)
        ones = sb("ones", [P, P], BF16)
        cst1 = sb("cst1", [P, CT_N])
        w1_gu = sb("w1_gu", [P, E1 * KH * GU_N])
        w1_dn = sb("w1_dn", [P, E1 * 2 * H])

        def carve(store, sizes):
            at, parts_of = 0, []
            for n in sizes:
                parts_of.append(store[:, at:at + n])
                at += n
            return parts_of
        wsel8, wblk, comb_b0, comb_b1, combT, small, *prod = carve(
            w1_gu, [NT * S * SUBJ, NT * P, N, N, N, SM_SPLIT] + [HALF] * 4)
        wsel8 = wsel8.rearrange("p (t d j) -> p t d j", t=NT, d=S)
        wblk = wblk.rearrange("p (t b d) -> p t b d", t=NT, b=BG)
        comb_b = [comb_b0, comb_b1]
        x_tok, la, _, slot_store = carve(w1_dn, [E1 * 2 * H // WD_PIECES] * WD_PIECES)
        x_tok = x_tok.rearrange("p (t h) -> p t h", t=NT)
        zeros = la
        la = la.rearrange("p (j n) -> p j n", j=2)
        la_hi = sb("la_hi", [P, 2, N], F32R)
        la_lo = sb("la_lo", [P, 2, N], F32R)
        small_hi = sb("small_hi", [P, SM_SPLIT], F32R)
        small_lo = sb("small_lo", [P, SM_SPLIT], F32R)
        routers = sb("routers", [P, R_N])
        wsub = sb("wsub", [P, SUBJ, S])
        xT = sb("xT", [P, KH, N])
        act_f = sb("act_f", [P, KH, N])
        act_hi = sb("act_hi", [P, KH, N], F32R)
        act_lo = sb("act_lo", [P, KH, N], F32R)
        idx_ti = sb("idx_ti", [P, NT], I32)
        idx_t = sb("idx_t", [P, NT])
        subj_oh = sb("subj_oh", [P, NT, SUBJ])
        wsel = sb("wsel", [P, NT, S])
        lmask = sb("lmask", [P, B])
        r_max = sb("r_max", [P, NT])
        r_lg = sb("r_lg", [P, NT, E1 + 1])
        r_ex = sb("r_ex", [P, NT, E1 + 1])
        r_logit = sb("r_logit", [P, NT, LOGIT1])
        r_sum = sb("r_sum", [P, NT])
        r_rec = sb("r_rec", [P, NT])
        r_gate = sb("r_gate", [P, NT, E1])
        r_top = sb("r_top", [P, NT, 8])
        r_idx = sb("r_idx", [P, NT, 8], U32)
        r_idf = sb("r_idf", [P, NT, 8])
        r_oh = sb("r_oh", [P, K1, NT, E1])
        r_ohb = sb("r_ohb", [P, K0, NT, E0], BF16)
        r_kept = sb("r_kept", [P, K1, NT, E1])
        comb = sb("comb", [P, NT, E0])
        sg = sb("sg", [P, NT])
        sg_b = sb("sg_b", [P, N])
        multi = sb("multi", [P, NT, E1], BF16)
        r_cmp = sb("r_cmp", [P, E1, E1])
        r_thr = sb("r_thr", [P, E1, NT])
        tiles = sb("tiles", [P, E1])
        ahead = sb("ahead", [P, E1])
        upto = sb("upto", [P, E1])
        first = sb("first", [P, E1])
        slot = sb("slot", [P, NT, E1])
        slot_k = sb("slot_k", [P, K1, NT])
        slot_i = sb("slot_i", [P, K1, NT], I32)
        tile_i = sb("tile_i", [P, K1, NT], I32)
        row_i = sb("row_i", [P, K1, NT], I32)
        tile_k = sb("tile_k", [P, K1, NT])
        row_k = sb("row_k", [P, K1, NT])
        own_cmp = sb("own_cmp", [1, SLOT_TILES, E1])
        own_f = sb("own_f", [1, SLOT_TILES])
        own = sb("own", [1, SLOT_TILES], I32)
        empty = sb("empty", [P, SLOT_TILES])
        get_f = sb("get_f", [P, SLOT_TILES])
        put_f = sb("put_f", [P, SLOT_TILES])
        slot_w = sb("slot_w", [P, SLOT_TILES])
        get = [sb(f"get{i}", [P, 1], U32) for i in range(RING)]
        put = [sb(f"put{i}", [P, 1], U32) for i in range(RING)]
        w_raw = [sb(f"w_raw{i}", [P, WMAX]) for i in range(2)]
        w_hi = [sb(f"w_hi{i}", [P, WMAX], F32R) for i in range(2)]
        w_lo = [sb(f"w_lo{i}", [P, WMAX], F32R) for i in range(2)]
        silu = [sb(f"silu{i}", [P, HALF]) for i in range(2)]
        hid = [sb(f"hid{i}", [P, HALF]) for i in range(2)]
        hid_hi = [sb(f"hid_hi{i}", [P, HALF], F32R) for i in range(2)]
        hid_lo = [sb(f"hid_lo{i}", [P, HALF], F32R) for i in range(2)]
        oh_row = [v.rearrange("p (t r) -> p t r", t=NT) for v in carve(act_f[:].rearrange("p k n -> p (k n)"), [NT * P] * 2)]
        oh_val0, oh_val1, oh_tile = carve(slot_store, [NT * ROUTE_N] * 2 + [NT * SLOT_TILES])
        oh_val = [v.rearrange("p (t c) -> p t c", t=NT) for v in (oh_val0, oh_val1)]
        oh_tile = oh_tile.rearrange("p (t c) -> p t c", t=NT)
        wide = slice(WIDTH[SH], WIDTH[SH] + H)
        xg = [w_raw[0][:, wide], w_raw[1][:, wide]] + carve(sb("xg", [P, 2 * H]), [H] * 2)
        xgT = [sb(f"xgT{i}", [P, KH, P]) for i in range(2)]
        t_silu = [silu[i][:, 0:I_EXP] for i in range(2)]
        t_hid = [hid[i][:, 0:I_EXP] for i in range(2)]
        t_hidT = [sb(f"t_hidT{i}", [HALF_I, 2, P]) for i in range(2)]
        t_out = [w_raw[i // 2][:, (i % 2) * H:(i % 2 + 1) * H] for i in range(RING)]
        base = act_f[:].rearrange("p k n -> p (k n)").rearrange("p (t h) -> p t h", t=NT)

        def bank(name):
            return ctx.enter_context(nc.psum_tensor(name, [P, 512], F32))
        Y = [[bank(f"y{m}{s}") for s in range(2)] for m in range(KH)]
        GU = [[bank(f"gu{s}{j}") for j in range(2)] for s in range(2)]
        HA = GU[1]
        logit_ps, rank_ps, combT_ps = GU[1][0], Y[0][1], Y[1]
        ROUTE, turn_ps = GU[1]
        at = np.cumsum([0, NT * LOGIT1, NT * E1, E1, ROUTE_N])
        logit1_ps, rank1_ps, count_ps, slot_ps = (ROUTE[:, a:b] for a, b in zip(at[:-1].tolist(), at[1:].tolist()))
        xgT_ps = [GU[1][1][:, i * H:(i + 1) * H] for i in range(2)]
        gu_ps = [GU[0][i][:, 0:GU_N] for i in range(2)]
        hidT_ps = [GU[1][0][0:HALF_I, i * H:(i + 1) * H] for i in range(2)]
        out_ps = [Y[0][i][:, 0:H] for i in range(2)]

        s_in = {k: sem("in_" + k) for k in ("cst", "idx", "small", "wsub", "xtok0", "xtok1", "xT", "cst0", "cst1", "routers", "idx_t")}
        s_raw = [sem(f"raw_landed{i}") for i in range(2)]
        s_comb = [sem(f"comb_landed{i}") for i in range(2)]
        s_scr = sem("scratch_written")
        s_zero, s_yb = sem("zeros_ready"), sem("y_b_zeroed")
        s_w1 = sem("w1_landed")
        s_x2t, s_x2c, s_x2 = sem("x2_turned"), sem("x2_in_sbuf"), sem("x2_in_dram")
        s_ohs, s_slot, s_ids = sem("slot_onehots"), sem("slots_done"), sem("ids_ready")
        s_sgp, s_sgb = sem("sg_spread"), sem("sg_in_sbuf")
        s_bt, s_bc, s_base = sem("base_turned"), sem("base_in_sbuf"), sem("base_in_out")
        t_get = sem("get_ready")
        t_in = [sem(f"tile_landed{i}") for i in range(RING)]
        t_xT, t_xTs = sem("tile_turned"), sem("tile_turned_sbuf")
        t_gu, t_act, t_hd = sem("tile_gate_up"), sem("tile_silu"), sem("tile_hid")
        t_hT, t_hTs = sem("tile_hid_turned"), sem("tile_hid_sbuf")
        t_dn, t_put = sem("tile_down"), sem("tile_out_ready")
        s_acc = [sem("y_b_added"), sem("out_added")]
        s_held = sem("pool_held")
        s_out = sem("out_written")
        s_whi, s_whd = sem("w_hi_ready"), sem("w_hi_down_ready")
        s_wg, s_w = sem("w_gate_up_split"), sem("w_split")
        s_small = sem("small_split")
        s_g, s_u, s_d = sem("gate_done"), sem("up_done"), sem("down_done")
        s_silu, s_prod, s_h = sem("silu_done"), sem("prod_done"), sem("hid_done")
        s_hh, s_hl = sem("hid_hi_done"), sem("hid_lo_done")
        s_chain = sem("dve_chain")
        s_soh, s_ws8 = sem("subjects_ready"), sem("half_selected")
        s_blk, s_xc = sem("wblk_ready"), sem("cond0_done")
        s_x1 = sem("x1_ready")
        s_actf, s_acth, s_actl = sem("act_f_ready"), sem("act_hi_ready"), sem("act_lo_ready")
        s_cb16 = sem("consts_ready")
        s_logit, s_lgc, s_rlg, s_exp = sem("logits_done"), sem("logits_read"), sem("shifted_ready"), sem("exp_done")
        s_oh, s_rank = sem("onehot_ready"), sem("rank_done")
        s_cmb, s_cmbT, s_cmbS = sem("comb_ready"), sem("combT_done"), sem("combT_in_sbuf")
        s_la, s_lam, s_lah, s_lal = sem("lora_done"), sem("lora_masked"), sem("lora_hi"), sem("lora_lo")
        s_bd, s_ha = sem("cond_done"), sem("lora_down_done")
        s_res = sem("residual_out")

        block = ctx.enter_context(nc.Block())

        def half(s):
            return slice(s * HALF, (s + 1) * HALF)

        COMB0 = [16 * len({r // I_EXP for r in range(c * P, (c + 1) * P)}) for c in range(2)]

        def pair(st, n, s):
            return GU[s if st == L0 or isinstance(n, int) and n == 2 * C0[COND] + 1 else 0]

        def run_tiles(eng, step):
            body = (SLOT_TILES - RING - AHEAD) // RING
            for i in range(RING):
                step(i, i)
            with eng.Fori(0, body) as r:
                for j in range(RING):
                    step(RING + j + RING * r, j)
            for i in range(RING + RING * body, SLOT_TILES):
                step(i, i % RING)

        def gu_cols(st):
            return slice(0, 2 * KIN[st] * P)

        def dn_cols(st):
            return slice(2 * KIN[st] * P, WIDTH[st])

        def select_subject(eng, t):
            dim = [P, t.stop - t.start, S, SUBJ]
            return eng.tensor_tensor(wsel8[:, t], wsub[:].rearrange("p s d -> p d s").unsqueeze(1).broadcast_to(dim),
                                     subj_oh[:, t].unsqueeze(2).broadcast_to(dim), ALU.mult)

        def rows(tail):
            return slice(SH_TAIL if tail else 0, P)

        def tile(i):
            return bass.ds(i, 1)

        def isa(i, lo):
            return not isinstance(i, int) or i >= lo

        def below(i, hi):
            return not isinstance(i, int) or i < hi

        def run_chunks(eng, st, first, last, chunk):
            pairs = (last - first) // 2
            if pairs > 1:
                with eng.Fori(0, pairs) as i:
                    for k in range(2):
                        chunk(C0[st] + first + k + 2 * i, (C0[st] + first + k) % 2)
                first += 2 * pairs
            for c in range(first, last):
                chunk(C0[st] + c, (C0[st] + c) % 2)

        def wait_pos(eng, s, v):
            if not isinstance(v, int) or v > 0:
                eng.wait_ge(s, v)

        @block.sync
        def _(sp):
            sp.dma_start(idx_ti[:], d["idx_t"]).then_inc(s_in["idx_t"], 16)
            sp.dma_start(cst0[:], d["cst0"]).then_inc(s_in["cst0"], 16)
            sp.dma_start(wsub[:], d["wsub"]).then_inc(s_in["wsub"], 16)
            sp.dma_start(x_tok[:, 0:NT // 2], d["x_tok"][:, 0:NT // 2]).then_inc(s_in["xtok0"], 16)
            sp.dma_start(x_tok[:, NT // 2:], d["x_tok"][:, NT // 2:]).then_inc(s_in["xtok1"], 16)

            def raw(st, c, par):
                wait_pos(sp, s_w, c - 1)
                sp.dma_start(w_raw[par][:, 0:WIDTH[st]], d["w"][st][bass.ds(c - C0[st], 1)]
                             .rearrange("a p n -> (a p) n")).then_inc(s_raw[par], 16)

            def raw_first(st):
                for c in range(C0[st], C0[st] + 2):
                    raw(st, c, c % 2)

            def combs(st, c, par):
                wait_pos(sp, s_h, 2 * c - 2)
                sp.dma_start(comb_b[par][:],
                             d["scr"][bass.ds((c - C0[st]) * (P // GRP), P // GRP)]
                             .unsqueeze(1).broadcast_to([P // GRP, GRP, N])).then_inc(s_comb[par], 16)

            raw_first(L0)
            sp.dma_start(idx_i[:], d["idx"].broadcast_to([P, B])).then_inc(s_in["idx"], 16)
            sp.dma_start(cst[:], d["cst"]).then_inc(s_in["cst"], 16)
            sp.dma_start(routers[:], d["routers"]).then_inc(s_in["routers"], 16)
            sp.dma_start(small, d["small"]).then_inc(s_in["small"], 16)
            for c in range(2, 4):
                raw(L0, c, c % 2)
            sp.dma_start(xT[:], d["xT"]).then_inc(s_in["xT"], 16)
            sp.wait_ge(s_cmbS, 1)
            for c in range(2):
                for e in range(E0):
                    a, b = (min(max(r - c * P, 0), P) for r in (e * I_EXP, (e + 1) * I_EXP))
                    if a < b:
                        sp.dma_start(comb_b[c][a:b], combT[e:e + 1, :].unsqueeze(1).broadcast_to([1, b - a, N])
                                     ).then_inc(s_comb[c], 16)
            sp.dma_start(d["scr"].rearrange("(e g) n -> e g n", g=GPE),
                         combT[0:E0, :].unsqueeze(1).broadcast_to([E0, GPE, N])).then_inc(s_scr, 16)
            sp.wait_ge(s_scr, 16)

            def l0_chunk(c, par):
                combs(L0, c, par)
                raw(L0, c + 2, par)
            run_chunks(sp, L0, 2, NC[L0] - 2, l0_chunk)
            for c in range(NC[L0] - 2, NC[L0]):
                combs(L0, c, c % 2)
            sp.dma_start(cst1[:], d["cst1"]).then_inc(s_in["cst1"], 16)
            sp.wait_ge(s_zero, 1)
            sp.dma_start(d["y_b"].rearrange("(p t) h -> p (t h)", p=P), zeros).then_inc(s_yb, 16)

            raw_first(COND)
            sp.wait_ge(s_h, 2 * NC[L0])

            def w1_piece(k):
                n = W1_EXP * KH * GU_N
                sp.dma_start(w1_gu[:, bass.ds(k * n, n)], d["w1_gu"][:, bass.ds(k * n, n)]).then_inc(s_w1, 16)

            def cond_chunk(c, par):
                raw(COND, c, par)
                w1_piece(c - C0[COND])
            for k in range(2):
                w1_piece(k)
            run_chunks(sp, COND, 2, NC[COND], cond_chunk)
            raw_first(SH)
            for c in range(C0[SH] + 2, C0[SH] + 4):
                raw(SH, c, c % 2)
            sp.wait_ge(s_x2c, 4)
            sp.dma_start(d["x2"].rearrange("(t p) h -> p t h", p=P), x_tok[:]).then_inc(s_x2, 16)
            sp.wait_ge(s_bd, 2)
            sp.wait_ge(s_x2, 16)
            for k in range(WD_PIECES):
                if k >= 2:
                    raw(SH, C0[SH] + 2 + k, (C0[SH] + k) % 2)
                if k == WD_PIECES - 1:
                    sp.wait_ge(s_slot, K1)
                n = WD_EXP * 2 * H
                sp.dma_start(w1_dn[0:HALF_I, k * n:(k + 1) * n], d["w1_dn"][:, k * n:(k + 1) * n]).then_inc(s_w1, 16)
            out_tok = d["out"].rearrange("(t p) h -> p t h", p=P)
            for s in range(2):
                t = slice(s * NT // 2, (s + 1) * NT // 2)
                sp.wait_ge(s_bc, KH * (s + 1))
                sp.dma_start(out_tok[:, t], base[:, t]).then_inc(s_base, 16)
            sp.wait_ge(s_out, 16)

        @block.gpsimd
        def _(pool):
            nc.gpsimd.memset(zeros, 0.0).then_inc(s_zero, 1)
            pool.wait_ge(s_in["wsub"], 16)
            pool.wait_ge(s_soh, 1)
            select_subject(nc.gpsimd, slice(NT // 2, NT)).then_inc(s_ws8, 1)

            def low(st, c, par):
                for rounded, split, w in ((s_whi, s_wg, gu_cols(st)), (s_whd, s_w, dn_cols(st))):
                    pool.wait_ge(rounded, c + 1)
                    nc.gpsimd.tensor_tensor(w_lo[par][:, w], w_raw[par][:, w], w_hi[par][:, w].bitcast(F32),
                                            ALU.subtract).then_inc(split, 1)

            low(L0, 0, 0)
            low(L0, 1, 1)
            pool.wait_ge(s_in["small"], 16)
            nc.gpsimd.tensor_copy(small_hi[:], small).then_inc(s_small, 1)
            pool.wait_ge(s_small, 1)
            nc.gpsimd.tensor_tensor(small_lo[:], small, small_hi[:].bitcast(F32),
                                    ALU.subtract).then_inc(s_small, 1)
            for st in STAGES:
                run_chunks(pool, st, 2 if st == L0 else 0, NC[st], lambda c, par: low(st, c, par))

            def hold(sem_of, v):
                pool.wait_ge(sem_of, v)
                pool.sem_inc(s_held, 1)

            def gather(i, j):
                hold(t_get, i + 1)
                nc.gpsimd.indirect_dma_start(xg[j], None, d["x2"], bass.IndirectOffsetOnAxis(ap=get[j][:], axis=0)
                                             ).then_inc(t_in[j], 16)

            def scatter(i, j):
                par = j % 2
                hold(t_put, i + 1)
                if isa(i, 2):
                    hold(s_acc[par], 8 * (i - par))
                elif i == 1:
                    pool.wait_ge(s_base, 32)
                nc.gpsimd.indirect_dma_start((d["y_b"], d["out"])[par],
                                             bass.IndirectOffsetOnAxis(ap=put[j][:], axis=0), t_out[j], None,
                                             bounds_check=N - 1, oob_is_err=False, compute_op=ALU.add
                                             ).then_inc(s_acc[par], 16)

            def step(i, j):
                scatter(i, j)
                if below(i, SLOT_TILES - AHEAD):
                    gather(i + AHEAD, (j + AHEAD) % RING)

            pool.wait_ge(s_yb, 16)
            pool.wait_ge(s_x2, 16)
            for i in range(AHEAD):
                gather(i, i % RING)
            run_tiles(pool, step)
            pool.wait_ge(s_acc[0], 16 * ((SLOT_TILES + 1) // 2))
            pool.wait_ge(s_acc[1], 16 * (SLOT_TILES // 2))
            nc.gpsimd.dma_start(d["out"].rearrange("(p t) h -> p (t h)", p=P),
                                d["y_b"].rearrange("(p t) h -> p (t h)", p=P), accum_op=ALU.add, max_dma_last_dim=NT * H * 4
                                ).then_inc(s_out, 16)

        @block.scalar
        def _(act):
            A = nc.scalar

            def round_gate_up(st, c, par):
                act.wait_ge(s_raw[par], 8 * (c - par) + 16)
                wait_pos(act, s_d if st == COND else s_u, 2 * c - 2)
                w = gu_cols(st)
                A.activation(w_hi[par][:, w], w_raw[par][:, w], ACT.Copy).then_inc(s_whi, 1)

            def round_down(st, c, par):
                wait_pos(act, s_d, 2 * c - 2)
                w = dn_cols(st)
                A.activation(w_hi[par][:, w], w_raw[par][:, w], ACT.Copy).then_inc(s_whd, 1)

            def round_weights(st, c, par):
                round_gate_up(st, c, par)
                round_down(st, c, par)

            def silu_of(st, n, s, tail=False):
                act.wait_ge(*((s_u, n + 1) if tail else (s_g, n + 1)))
                wait_pos(act, s_prod, n - 1)
                gate = pair(st, n, s)[0][0:SH_TAIL if tail else P]
                A.activation(silu[s][rows(tail)], gate, ACT.Silu).then_inc(s_silu, 1)

            def hid_high(st, n, s, tail=False):
                if st == L0:
                    act.wait_ge(s_h, n + 1)
                else:
                    act.wait_ge(s_prod, n + 1)
                wait_pos(act, s_d, n - 1)
                A.activation(hid_hi[s][rows(tail)], hid[s][rows(tail)], ACT.Copy).then_inc(s_hh, 1)

            def chunk_of(st, nxt=None):
                def chunk(c, par):
                    for s in range(2):
                        silu_of(st, 2 * c + s, s)
                        hid_high(st, 2 * c + s, s)
                        if s == (nxt == COND):
                            round_weights(st if nxt is None else nxt, c + 1, 1 - par)
                return chunk

            def units(st, first):
                run_chunks(act, st, first, NC[st] - 1, chunk_of(st))
                c = C0[st] + NC[st] - 1
                chunk_of(st, st + 1)(c, c % 2)

            round_weights(L0, 0, 0)
            round_weights(L0, 1, 1)
            for s in range(2):
                act.wait_ge(s_xc, s + 1)
                for m in range(KH):
                    A.activation(act_f[:, m, half(s)], Y[m][s][:], ACT.Copy).then_inc(s_actf, 1)
            for s in range(2):
                for m in range(KH):
                    act.wait_ge(s_actf, s * KH + m + 1)
                    A.activation(act_hi[:, m, half(s)], act_f[:, m, half(s)], ACT.Copy).then_inc(s_acth, 1)
            act.wait_ge(s_rlg, 1)
            A.activation(r_ex[:, :, 0:E0], r_lg[:, :, 0:E0], ACT.Exp).then_inc(s_exp, 1)
            for n in range(4):
                silu_of(L0, n, n % 2)
                if n == 2:
                    round_gate_up(L0, 2, 0)
            for n in range(4):
                hid_high(L0, n, n % 2)
            round_down(L0, 2, 0)
            units(L0, 2)
            for s in range(2):
                for m in range(KH):
                    act.wait_ge(s_x1, s * KH + m + 1)
                    A.activation(act_hi[:, m, half(s)], xT[:, m, half(s)], ACT.Copy).then_inc(s_acth, 1)
            for s in range(2):
                for j in range(2):
                    act.wait_ge(s_lam, 2 * s + j + 1)
                    A.activation(la_hi[:, j, half(s)], la[:, j, half(s)], ACT.Copy).then_inc(s_lah, 1)
            chunk_of(COND)(C0[COND], C0[COND] % 2)
            units(COND, 1)
            for s in range(2):
                act.wait_ge(s_lam, 4 + s + 1)
                A.activation(la_hi[:, 0, half(s)], la[:, 0, half(s)], ACT.Copy).then_inc(s_lah, 1)
            for s in range(2):
                act.wait_ge(s_bd, s + 1)
                for m in range(KH):
                    A.activation(act_hi[:, m, half(s)], Y[m][s][:], ACT.Copy).then_inc(s_acth, 1)
            for s in range(2):
                for m in range(KH):
                    act.wait_ge(s_actl, 4 * KH + s * KH + m + 1)
                    A.activation(act_f[:, m, half(s)], Y[m][s][:], ACT.Copy).then_inc(s_actf, 1)
            c = C0[SH]

            def turned(b):
                act.wait_ge(s_x2t, b + 1)
                A.activation(x_tok[:, 2 * b:2 * b + 2].rearrange("p t h -> p (t h)"), turn_ps[:],
                             ACT.Copy).then_inc(s_x2c, 1)

            def gate_spread(s):
                act.wait_ge(s_sgp, s + 1)
                A.activation(sg_b[:, half(s)], turn_ps[:], ACT.Copy).then_inc(s_sgb, 1)

            def turned_in(i, par):
                act.wait_ge(t_xT, i + 1)
                if isa(i, 2):
                    act.wait_ge(t_gu, i - 1)
                A.activation(xgT[par][:].rearrange("p k n -> p (k n)"), xgT_ps[par], ACT.Copy).then_inc(t_xTs, 1)

            between = {0: lambda: turned(0), 1: lambda: turned(1), 2: lambda: turned(2), 3: lambda: turned(3),
                       4: lambda: gate_spread(0), 5: lambda: gate_spread(1)}
            for n in range(2 * NC[SH]):
                s, k = n % 2, c + n // 2
                tail = n // 2 == NC[SH] - 1
                silu_of(SH, 2 * c + n, s, tail)
                if n == 2 * NC[SH] - 1:
                    turned_in(0, 0)
                hid_high(SH, 2 * c + n, s, tail)
                if s == 0 and n // 2 + 1 < NC[SH]:
                    round_weights(SH, k + 1, (k + 1) % 2)
                if n == 0:
                    act.wait_ge(s_rlg, 2)
                    A.activation(r_ex[:], r_lg[:], ACT.Exp).then_inc(s_exp, 1)
                elif n - 1 in between:
                    between[n - 1]()

            def step(i, j):
                par = j % 2
                act.wait_ge(t_gu, i + 1)
                if isa(i, 2):
                    act.wait_ge(t_hd, i - 1)
                A.activation(t_silu[par], gu_ps[par][:, 0:I_EXP], ACT.Silu).then_inc(t_act, 1)
                if below(i, SLOT_TILES - 1):
                    turned_in(i + 1, 1 - par)
                if isinstance(i, int) and 1 <= i < 3:
                    act.wait_ge(s_bt, i)
                    for b in range(2):
                        t = (i - 1) * NT // 2 + 2 * b
                        A.activation(base[:, t:t + 2].rearrange("p t h -> p (t h)"), Y[b][i - 1][:],
                                     ACT.Copy).then_inc(s_bc, 1)

            run_tiles(act, step)

        @block.vector
        def _(dve):
            count = [0]

            def chain(ins):
                count[0] += 1
                ins.then_inc(s_chain, 1)
                dve.wait_ge(s_chain, count[0])

            V = nc.vector
            blkm = cst0[:, CI_BLK:CI_BLK + BG]
            dve.wait_ge(s_in["idx_t"], 16)
            chain(V.tensor_copy(idx_t[:], idx_ti[:]))
            dve.wait_ge(s_in["cst0"], 16)
            V.tensor_tensor(subj_oh[:], cst0[:, CI_IOTA:CI_IOTA + SUBJ].unsqueeze(1).broadcast_to([P, NT, SUBJ]),
                            idx_t[:].unsqueeze(2).broadcast_to([P, NT, SUBJ]), ALU.is_equal).then_inc(s_soh, 1)
            dve.wait_ge(s_soh, 1)
            dve.wait_ge(s_in["wsub"], 16)
            for q in range(4):
                t = slice(q * NT // 4, (q + 1) * NT // 4)
                if q < 2:
                    chain(select_subject(V, t))
                else:
                    dve.wait_ge(s_ws8, 1)
                chain(V.reduce_sum(wsel[:, t], wsel8[:, t], axis=AX_X))
                dim = [P, NT // 4, BG, S]
                V.tensor_tensor(wblk[:, t], wsel[:, t].unsqueeze(2).broadcast_to(dim),
                                blkm.unsqueeze(1).unsqueeze(3).broadcast_to(dim), ALU.mult).then_inc(s_blk, 1)
            dve.wait_ge(s_in["idx"], 16)
            chain(V.tensor_copy(idx_f[:], idx_i[:]))
            V.tensor_scalar(lmask[:], idx_f[:], cst0[:, CI_AD:CI_AD + 1], None, ALU.is_equal).then_inc(s_cb16, 1)
            dve.wait_ge(s_in["cst"], 16)
            V.tensor_copy(tri[:], cst[:, CS_TRI:CS_TRI + P]).then_inc(s_cb16, 1)
            V.memset(ones[:], 1.0).then_inc(s_cb16, 1)

            def act_low(base, src):
                for s in range(2):
                    for m in range(KH):
                        dve.wait_ge(s_acth, base + s * KH + m + 1)
                        V.tensor_tensor(act_lo[:, m, half(s)], src(m, s), act_hi[:, m, half(s)].bitcast(F32),
                                        ALU.subtract).then_inc(s_actl, 1)

            def shift(lg, ne):
                chain(V.reduce_max(r_max[:], lg, axis=AX_X))
                return V.tensor_tensor(r_lg[:, :, 0:ne], lg, r_max[:].unsqueeze(2).broadcast_to([P, NT, ne]),
                                       ALU.subtract)

            def softmax(ne, j):
                dve.wait_ge(s_exp, j)
                chain(V.reduce_sum(r_sum[:], r_ex[:, :, 0:ne], axis=AX_X))
                chain(V.reciprocal(r_rec[:], r_sum[:]))
                chain(V.tensor_tensor(r_gate[:, :, 0:ne], r_ex[:, :, 0:ne],
                                      r_rec[:].unsqueeze(2).broadcast_to([P, NT, ne]), ALU.mult))

            def top(ne):
                for t in range(NT):
                    ins = V.max(r_top[:, t, :], r_gate[:, t, 0:ne])
                chain(ins)
                for t in range(NT):
                    ins = V.max_index(r_idx[:, t, :], r_top[:, t, :], r_gate[:, t, 0:ne])
                chain(ins)
                chain(V.tensor_copy(r_idf[:], r_idx[:]))

            def onehot(out, ne, k):
                iota = cst0[:, CI_IOTA:CI_IOTA + ne].unsqueeze(1).broadcast_to([P, NT, ne])
                return V.tensor_tensor(out[:, k, :, 0:ne], iota,
                                       r_idf[:, :, k].unsqueeze(2).broadcast_to([P, NT, ne]), ALU.is_equal)

            def comb_out():
                for s in range(2):
                    dve.wait_ge(s_cmbT, s + 1)
                    ins = V.tensor_copy(combT[0:E0, half(s)], combT_ps[s][0:E0, :])
                ins.then_inc(s_cmbS, 1)

            def product(st, n, s, out, tail=False):
                dve.wait_ge(s_u, n + 1)
                dve.wait_ge(s_silu, n + 1)
                up = pair(st, n, s)[0 if tail else 1]
                V.tensor_tensor(out[rows(tail)], silu[s][rows(tail)], up[rows(tail)], ALU.mult).then_inc(s_prod, 1)

            def weigh(st, c, par, s, src):
                dve.wait_ge(s_prod, 2 * c + s + 1)
                dve.wait_ge(s_comb[par], 8 * (c - par) + COMB0[par])
                V.tensor_tensor(hid[s][:], src[:], comb_b[par][:, half(s)], ALU.mult).then_inc(s_h, 1)

            def hid_low(n, s, tail=False):
                dve.wait_ge(s_hh, n + 1)
                wait_pos(dve, s_d, n - 1)
                V.tensor_tensor(hid_lo[s][rows(tail)], hid[s][rows(tail)], hid_hi[s][rows(tail)].bitcast(F32),
                                ALU.subtract).then_inc(s_hl, 1)

            def unit(st, c, par, s, tail=False):
                n = 2 * c + s
                product(st, n, s, prod[s] if st == L0 else hid[s], tail)
                if st == L0:
                    weigh(st, c, par, s, prod[s])
                hid_low(n, s, tail)

            def units(st, first):
                run_chunks(dve, st, first, NC[st], lambda c, par: [unit(st, c, par, s) for s in range(2)])

            act_low(0, lambda m, s: act_f[:, m, half(s)])
            dve.wait_ge(s_logit, 1)
            shift(logit_ps[:, 0:NT * E0].rearrange("p (t e) -> p t e", t=NT), E0).then_inc(s_rlg, 1)
            softmax(E0, 1)
            top(E0)
            onehot(r_ohb, E0, 0)
            onehot(r_ohb, E0, 1).then_inc(s_oh, 1)
            product(L0, 0, 0, prod[0])
            dve.wait_ge(s_oh, 1)
            dve.wait_ge(s_rank, 1)
            rank = rank_ps[:, 0:K0 * NT * E0].rearrange("p (k t e) -> p k t e", k=K0, t=NT)
            for k in range(K0):
                ins = V.scalar_tensor_tensor(out=r_kept[:, k, :, 0:E0], in0=rank[:, k], scalar=float(CAP),
                                             in1=r_ohb[:, k], op0=ALU.is_le, op1=ALU.mult)
            chain(ins)
            for k in range(K0):
                ins = V.tensor_tensor(r_oh[:, k, :, 0:E0], r_kept[:, k, :, 0:E0],
                                      r_top[:, :, k].unsqueeze(2).broadcast_to([P, NT, E0]), ALU.mult)
            chain(ins)
            V.tensor_tensor(comb[:, :, 0:E0], r_oh[:, 0, :, 0:E0], r_oh[:, 1, :, 0:E0], ALU.add).then_inc(s_cmb, 1)
            comb_out()
            product(L0, 1, 1, prod[1])
            product(L0, 2, 0, prod[2])
            for s in range(2):
                weigh(L0, 0, 0, s, prod[s])
            for s in range(2):
                hid_low(s, s)
            product(L0, 3, 1, prod[3])
            dve.wait_ge(s_hl, 2)
            for s in range(2):
                weigh(L0, 1, 1, s, prod[2 + s])
            for s in range(2):
                hid_low(2 + s, s)
            units(L0, 2)

            dve.wait_ge(s_in["xT"], 16)
            for s in range(2):
                dve.wait_ge(s_d, 2 * C0[COND] - 1 + s)
                for m in range(KH):
                    V.tensor_tensor(xT[:, m, half(s)], xT[:, m, half(s)], Y[m][s][:], ALU.add).then_inc(s_x1, 1)
                for m in range(KH):
                    dve.wait_ge(s_acth, 4 + s * KH + m + 1)
                    V.tensor_tensor(act_lo[:, m, half(s)], xT[:, m, half(s)], act_hi[:, m, half(s)].bitcast(F32),
                                    ALU.subtract).then_inc(s_actl, 1)

            dve.wait_ge(s_yb, 16)

            dve.wait_ge(s_cb16, 3)

            def keep_adapter(j, s, ps):
                mask = lmask[:, s * B // 2:(s + 1) * B // 2].unsqueeze(2).broadcast_to([P, B // 2, S])
                V.tensor_tensor(la[:, j, half(s)].rearrange("p (b t) -> p b t", t=S),
                                ps[:].rearrange("p (b t) -> p b t", t=S), mask, ALU.mult).then_inc(s_lam, 1)

            def lora_low(j, s, done):
                dve.wait_ge(s_lah, done)
                V.tensor_tensor(la_lo[:, j, half(s)], la[:, j, half(s)], la_hi[:, j, half(s)].bitcast(F32),
                                ALU.subtract).then_inc(s_lal, 1)

            for s in range(2):
                for j in range(2):
                    dve.wait_ge(s_la, 2 * s + j + 1)
                    keep_adapter(j, s, Y[j][s])
                for j in range(2):
                    lora_low(j, s, 2 * s + j + 1)
            for s in range(2):
                unit(COND, C0[COND], C0[COND] % 2, s)
            units(COND, 1)
            for s in range(2):
                dve.wait_ge(s_ha, s + 1)
                keep_adapter(0, s, HA[s])
                lora_low(0, s, 4 + s + 1)

            act_low(8, lambda m, s: Y[m][s][:])
            c = C0[SH]
            unit(SH, c, c % 2, 0)
            dve.wait_ge(s_logit, 2)
            chain(V.tensor_copy(r_logit[:], logit1_ps.rearrange("p (t e) -> p t e", t=NT)))
            V.tensor_scalar(r_lg[:, :, E1], r_logit[:, :, E1], -1.0, None, ALU.mult).then_inc(s_lgc, 1)
            shift(r_logit[:, :, 0:E1], E1).then_inc(s_rlg, 1)
            unit(SH, c, c % 2, 1)
            softmax(E1, 2)
            top(E1)
            unit(SH, c + 1, (c + 1) % 2, 0)
            for k in range(K1):
                ins = onehot(r_oh, E1, k)
            chain(ins)
            V.tensor_tensor(r_kept[:, 0], r_oh[:, 0], r_oh[:, 1], ALU.add)
            V.reduce_sum(r_sum[:], r_top[:, :, 0:K1], axis=AX_X)
            chain(V.tensor_tensor(r_kept[:, 1], r_oh[:, 2], r_oh[:, 3], ALU.add))
            V.tensor_tensor(multi[:], r_kept[:, 0], r_kept[:, 1], ALU.add).then_inc(s_oh, 1)
            V.tensor_scalar(r_max[:], r_ex[:, :, E1], 1.0, None, ALU.add)
            chain(V.tensor_scalar(r_sum[:], r_sum[:], 1e-9, None, ALU.max))
            V.reciprocal(sg[:], r_max[:]).then_inc(s_cmb, 1)
            chain(V.reciprocal(r_rec[:], r_sum[:]))
            V.tensor_tensor(r_top[:, :, 0:K1], r_top[:, :, 0:K1],
                            r_rec[:].unsqueeze(2).broadcast_to([P, NT, K1]), ALU.mult)
            unit(SH, c + 1, (c + 1) % 2, 1)
            dve.wait_ge(s_in["cst1"], 16)
            dve.wait_ge(s_rank, 2)
            dim = [P, E1, NT]
            chain(V.tensor_tensor(r_thr[:], count_ps.unsqueeze(2).broadcast_to(dim),
                                  cst1[:, CT_THR:CT_THR + NT].unsqueeze(1).broadcast_to(dim), ALU.is_gt))
            chain(V.reduce_sum(tiles[:], r_thr[:], axis=AX_X))
            chain(V.tensor_tensor(r_cmp[:], tiles[:].unsqueeze(1).broadcast_to([P, E1, E1]),
                                  cst1[:, CT_LT:CT_LT + E1 * E1].rearrange("p (e f) -> p e f", e=E1), ALU.mult))
            chain(V.reduce_sum(ahead[:], r_cmp[:], axis=AX_X))
            V.tensor_tensor(upto[:], ahead[:], tiles[:], ALU.add)
            chain(V.tensor_scalar(first[:], ahead[:], float(P), -1.0, ALU.mult, ALU.add))
            unit(SH, c + 2, c % 2, 0)
            chain(V.tensor_tensor(slot[:], rank1_ps.rearrange("p (t e) -> p t e", t=NT),
                                  first[:].unsqueeze(1).broadcast_to([P, NT, E1]), ALU.add))
            chain(V.tensor_tensor(r_kept[:].rearrange("p k t e -> p k (t e)"), r_oh[:].rearrange("p k t e -> p k (t e)"),
                                  slot[:].rearrange("p t e -> p (t e)").unsqueeze(1).broadcast_to([P, K1, NT * E1]),
                                  ALU.mult))
            chain(V.reduce_sum(slot_k[:], r_kept[:], axis=AX_X))
            chain(V.tensor_copy(slot_i[:], slot_k[:]))
            shift_by = P.bit_length() - 1
            V.tensor_scalar(tile_i[:], slot_i[:], shift_by, None, ALU.arith_shift_right)
            chain(V.tensor_scalar(row_i[:], slot_i[:], P - 1, None, ALU.bitwise_and))
            V.tensor_copy(tile_k[:], tile_i[:])
            chain(V.tensor_copy(row_k[:], row_i[:]))
            unit(SH, c + 2, c % 2, 1)

            def slot_onehots(k):
                if k >= 2:
                    dve.wait_ge(s_slot, k - 1)
                b, dim = k % 2, [P, NT, SLOT_TILES]
                V.tensor_tensor(oh_row[b], cst1[:, CT_ROW:CT_ROW + P].unsqueeze(1).broadcast_to([P, NT, P]),
                                row_k[:, k].unsqueeze(2).broadcast_to([P, NT, P]), ALU.is_equal)
                chain(V.tensor_tensor(oh_tile, cst1[:, CT_TILE:CT_TILE + SLOT_TILES].unsqueeze(1).broadcast_to(dim),
                                      tile_k[:, k].unsqueeze(2).broadcast_to(dim), ALU.is_equal))
                V.tensor_tensor(oh_val[b][:, :, 0:SLOT_TILES], oh_tile,
                                cst1[:, CT_TOK:CT_TOK + NT].unsqueeze(2).broadcast_to(dim), ALU.mult)
                V.tensor_tensor(oh_val[b][:, :, SLOT_TILES:], oh_tile,
                                r_top[:, :, k].unsqueeze(2).broadcast_to(dim), ALU.mult).then_inc(s_ohs, 1)

            for k in range(K1):
                slot_onehots(k)
                if k == 1:
                    dim = [1, SLOT_TILES, E1]
                    chain(V.tensor_tensor(own_cmp[:], cst1[0:1, CT_TILE:CT_TILE + SLOT_TILES].unsqueeze(2).broadcast_to(dim),
                                          upto[0:1, :].unsqueeze(1).broadcast_to(dim), ALU.is_ge))
                    chain(V.reduce_sum(own_f[:], own_cmp[:], axis=AX_X))
                    V.tensor_scalar(own[:], own_f[:], float(E1 - 1), None, ALU.min).then_inc(s_ids, 1)
                unit(SH, c + 3 + k // 2, (c + 3 + k // 2) % 2, k % 2)
            dve.wait_ge(s_slot, K1)
            got = slot_ps[:, 0:SLOT_TILES]
            V.tensor_scalar(get_f[:], got, -1.0, 0.0, ALU.add, ALU.max)
            V.tensor_copy(slot_w[:], slot_ps[:, SLOT_TILES:])
            chain(V.tensor_scalar(empty[:], got, 0.0, float(4 * N), ALU.is_equal, ALU.mult))
            chain(V.scalar_tensor_tensor(out=put_f[:], in0=got, scalar=-1.0, in1=empty[:], op0=ALU.add, op1=ALU.add))

            def tokens(i, j):
                if isa(i, RING):
                    dve.wait_ge(t_xT, i - RING + 1)
                V.tensor_scalar(get[j][:], get_f[:, tile(i)], 1.0, None, ALU.mult).then_inc(t_get, 1)

            for i in range(RING):
                tokens(i, i)
            for s in range(2):
                unit(SH, c + 5, (c + 5) % 2, s, tail=True)
            def base_half(s):
                part = base[:, s * NT // 2:(s + 1) * NT // 2].rearrange("p t h -> p (t h)")
                part = part.rearrange("p (m n) -> p m n", m=KH)
                dve.wait_ge(s_sgb, s + 1)
                dve.wait_ge(s_d, 2 * (C0[SH] + NC[SH]) - 1 + s)
                for m in range(KH):
                    ins = V.tensor_tensor(part[:, m], Y[m][s][:], sg_b[:, half(s)], ALU.mult)
                chain(ins)
                for m in range(KH):
                    V.tensor_tensor(xT[:, m, half(s)], xT[:, m, half(s)], part[:, m],
                                    ALU.add).then_inc(s_res, 1)

            base_half(0)
            def hidden(i, par):
                dve.wait_ge(t_act, i + 1)
                if isa(i, 2):
                    dve.wait_ge(t_hT, i - 1)
                V.tensor_tensor(t_hid[par], t_silu[par], gu_ps[par][:, I_EXP:GU_N], ALU.mult).then_inc(t_hd, 1)

            def output(i, j):
                dve.wait_ge(t_dn, i + 1)
                if isa(i, RING):
                    dve.wait_ge(s_acc[j % 2], 8 * (i - j % 2) - 16)
                V.tensor_scalar(put[j][:], put_f[:, tile(i)], 1.0, None, ALU.mult)
                V.tensor_scalar(t_out[j], out_ps[j % 2], slot_w[:, tile(i)], None, ALU.mult).then_inc(t_put, 1)

            def turned_hidden(i, par):
                dve.wait_ge(t_hT, SLOT_TILES if not below(i, SLOT_TILES - 2) else i + 1)
                if isa(i, 2):
                    dve.wait_ge(t_dn, i - 1)
                V.tensor_copy(t_hidT[par][:].rearrange("p k n -> p (k n)"), hidT_ps[par]).then_inc(t_hTs, 1)

            def step(i, j):
                hidden(i, j % 2)
                if isinstance(i, int) and i == 0:
                    base_half(1)
                if isa(i, 2):
                    output(i - 2, (j - 2) % RING)
                if isa(i, 1):
                    turned_hidden(i - 1, 1 - j % 2)
                if below(i, SLOT_TILES - RING):
                    tokens(i + RING, j)

            run_tiles(dve, step)
            last = SLOT_TILES - 1
            turned_hidden(last, last % 2)
            output(last - 1, (last - 1) % RING)
            output(last, last % RING)

        @block.tensor
        def _(pe):
            T = nc.tensor

            def mm3(out, w, x, start, stop):
                T.matmul(out, w[0], x[0], start=start, stop=False)
                T.matmul(out, w[0], x[1], start=False, stop=False)
                return T.matmul(out, w[1], x[0], start=False, stop=stop)

            def parts(t, *ix):
                return tuple(a[ix] for a in t)

            ACTV, SMALL, LA = (act_hi, act_lo), (small_hi, small_lo), (la_hi, la_lo)
            A = slice(None)

            for s in range(2):
                pe.wait_ge(s_in[f"xtok{s}"], 16)
                for t in range(s * NT // 2, (s + 1) * NT // 2):
                    pe.wait_ge(s_blk, t // 2 + 1)
                    for m in range(KH):
                        last = T.matmul(Y[m][s][:, (t % 4) * P:(t % 4 + 1) * P], x_tok[:, t, m * P:(m + 1) * P],
                                        wblk[:, t].rearrange("p b d -> p (b d)"), start=True, stop=True)
                last.then_inc(s_xc, 1)

            def logits(ps, done, off, ne):
                pe.wait_ge(s_in["routers"], 16)
                for t in range(NT):
                    if t % 4 == 0:
                        pe.wait_ge(s_actf, done + (t // 4 + 1) * KH)
                    for k in range(KH):
                        last = T.matmul(ps[:, t * ne:(t + 1) * ne], act_f[:, k, t * P:(t + 1) * P],
                                        routers[:, off + k * ne:off + (k + 1) * ne], start=k == 0, stop=k == KH - 1)
                last.then_inc(s_logit, 1)

            eye = cst[:, CS_ID:CS_ID + P]

            def comb_transposed():
                pe.wait_ge(s_cmb, 1)
                for t in range(NT):
                    ins = T.transpose(combT_ps[t // 4][0:E0, (t % 4) * P:(t % 4 + 1) * P], comb[:, t], eye)
                    if t % 4 == 3:
                        ins.then_inc(s_cmbT, 1)

            def ranks():
                pe.wait_ge(s_cb16, 3)
                pe.wait_ge(s_oh, 1)
                oh = r_ohb[:].rearrange("p k t e -> p (k t e)")
                total = K0 * NT * E0
                T.matmul(rank_ps[:, 0:total], tri[:], oh, start=True, stop=False)
                for b in range(1, K0 * NT):
                    last = T.matmul(rank_ps[:, b * E0:total], ones[:], oh[:, 0:total - b * E0], start=False,
                                    stop=b == K0 * NT - 1)
                last.then_inc(s_rank, 1)

            def gate_up(st, c, par, s, lora=False, between=None, tail=False):
                n, K = 2 * c + s, KIN[st]
                back = 2 if st == L0 else 1
                if s == 0:
                    pe.wait_ge(s_wg, c + 1)
                if not (lora and s == 1):
                    wait_pos(pe, s_silu, n + 1 - back)
                    wait_pos(pe, s_prod, n + 1 - back)
                if tail:
                    for k in range(K):
                        last = mm3(GU[0][0][:], parts((w_hi[par], w_lo[par]), A, slice(k * P, (k + 1) * P)),
                                   parts(ACTV, A, k, half(s)), k == 0, k == K - 1)
                    last.then_inc(s_u, 1)
                    return
                for j, done in ((0, s_g), (1, s_u)):
                    if j and between:
                        between()
                    for k in range(K):
                        if k == KH and lora:
                            pe.wait_ge(s_lal, 2 * s + j + 1)
                        x = parts(ACTV, A, k, half(s)) if k < KH else parts(LA, A, j, half(s))
                        off = (j * K + k) * P
                        last = mm3(pair(st, n, s)[j][:], parts((w_hi[par], w_lo[par]), A, slice(off, off + P)),
                                   x, k == 0, k == K - 1)
                    last.then_inc(done, 1)

            def down(st, c, par, s, start=False, stop=False, tail=False):
                n = 2 * c + s
                if s == 0:
                    pe.wait_ge(s_w, c + 1)
                pe.wait_ge(s_hh, n + 1)
                pe.wait_ge(s_hl, n + 1)
                order = (KH, 0, 1) if stop and st == COND else range(MOUT[st])
                for m in order:
                    if start and m == KH:
                        pe.wait_ge(s_prod, 2 * C0[COND] + 2)
                    off = (2 * KIN[st] + m) * P
                    closed = stop and (st != COND or m == KH)
                    last = mm3((Y[m][s] if m < KH else HA[s])[:], parts((w_hi[par], w_lo[par]), rows(tail), slice(off, off + P)),
                               parts((hid_hi[s], hid_lo[s]), rows(tail)), start, closed)
                    if stop and m == KH:
                        last.then_inc(s_ha, 1)
                last.then_inc(s_d, 1)

            def middle(st, c, par, start=False, stop=False):
                gate_up(st, c, par, 0)
                down(st, c - 1, 1 - par, 1, start=start)
                gate_up(st, c, par, 1)
                down(st, c, par, 0, stop=stop)

            def finish(st):
                c = C0[st] + NC[st] - 1
                if st == L0:
                    for s in range(2):
                        gate_up(st, c, c % 2, s)
                    down(st, c - 1, 1 - c % 2, 1)
                    down(st, c, c % 2, 0, stop=True)
                else:
                    middle(st, c, c % 2, stop=True)
                down(st, c, c % 2, 1, stop=True)

            logits(logit_ps, 0, SM_R0, E0)
            pe.wait_ge(s_actl, KH)
            gate_up(L0, 0, 0, 0)
            pe.wait_ge(s_actl, 2 * KH)
            pe.wait_ge(s_rlg, 1)
            gate_up(L0, 0, 0, 1, between=ranks)
            comb_transposed()
            gate_up(L0, 1, 1, 0)
            gate_up(L0, 1, 1, 1)
            gate_up(L0, 2, 0, 0)
            pe.wait_ge(s_cmbS, 1)
            for c in range(2):
                for s in range(2):
                    down(L0, c, c, s, start=c == 0)
            gate_up(L0, 2, 0, 1)
            down(L0, 2, 0, 0)
            run_chunks(pe, L0, 3, NC[L0] - 1, lambda c, par: middle(L0, c, par))
            finish(L0)

            pe.wait_ge(s_small, 2)
            for s in range(2):
                for j in range(2):
                    for k in range(KH):
                        if j == 0:
                            pe.wait_ge(s_actl, 2 * KH + KH * s + k + 1)
                        off = SM_A + (k * 2 + j) * P
                        last = mm3(Y[j][s][:], parts(SMALL, A, slice(off, off + P)), parts(ACTV, A, k, half(s)),
                                   k == 0, k == KH - 1)
                    last.then_inc(s_la, 1)
            c = C0[COND]
            gate_up(COND, c, c % 2, 0, lora=True)
            gate_up(COND, c, c % 2, 1, lora=True)
            down(COND, c, c % 2, 0, start=True)
            middle(COND, c + 1, (c + 1) % 2, start=True)
            run_chunks(pe, COND, 2, NC[COND] - 1, lambda c, par: middle(COND, c, par))
            finish(COND)
            for s in range(2):
                pe.wait_ge(s_lal, 4 + s + 1)
                for m in range(KH):
                    off = SM_BD + m * P
                    last = mm3(Y[m][s][:], parts(SMALL, A, slice(off, off + P)), parts(LA, A, 0, half(s)), False, True)
                last.then_inc(s_bd, 1)

            def ranks1():
                pe.wait_ge(s_oh, 2)
                oh = multi[:].rearrange("p t e -> p (t e)")
                total = NT * E1
                T.matmul(rank1_ps, tri[:], oh, start=True, stop=False)
                for b in range(1, NT):
                    T.matmul(rank1_ps[:, b * E1:total], ones[:], oh[:, 0:total - b * E1], start=False,
                             stop=b == NT - 1)
                for b in range(NT):
                    last = T.matmul(count_ps, ones[:], oh[:, b * E1:(b + 1) * E1], start=b == 0, stop=b == NT - 1)
                last.then_inc(s_rank, 1)

            def spread_gate(s):
                pe.wait_ge(s_cmb, 2)
                if s:
                    pe.wait_ge(s_sgb, s)
                else:
                    pe.wait_ge(s_x2c, 4)
                for t in range(4):
                    last = T.matmul(turn_ps[:, t * P:(t + 1) * P], sg[:, 4 * s + t:4 * s + t + 1].broadcast_to([P, P]), eye,
                                    start=True, stop=True)
                last.then_inc(s_sgp, 1)

            def slots(k):
                pe.wait_ge(s_ohs, k + 1)
                for t in range(NT):
                    last = T.matmul(slot_ps, oh_row[k % 2][:, t], oh_val[k % 2][:, t], start=k == 0 and t == 0,
                                    stop=k == K1 - 1 and t == NT - 1)
                last.then_inc(s_slot, 1)

            def turn_x2(b):
                if b:
                    pe.wait_ge(s_x2c, b)
                for t in range(2 * b, 2 * b + 2):
                    for m in range(KH):
                        last = T.transpose(turn_ps[:, (t % 2) * H + m * P:(t % 2) * H + (m + 1) * P],
                                           act_f[:, m, t * P:(t + 1) * P], eye)
                last.then_inc(s_x2t, 1)

            def turn_in(i, j):
                par = j % 2
                pe.wait_ge(t_in[j], 4 * (i - j) + 16)
                if isa(i, 2):
                    pe.wait_ge(t_xTs, i - 1)
                for k in range(KH):
                    last = T.transpose(xgT_ps[par][:, k * P:(k + 1) * P], xg[j][:, k * P:(k + 1) * P], eye)
                last.then_inc(t_xT, 1)

            c = C0[SH]
            pe.wait_ge(s_actl, 5 * KH)
            gate_up(SH, c, c % 2, 0)
            pe.wait_ge(s_actl, 6 * KH)
            logits(logit1_ps, 2 * KH, SM_R1, LOGIT1)
            turn_x2(0)
            gate_up(SH, c, c % 2, 1)
            pe.wait_ge(s_actf, 4 * KH)
            down(SH, c, c % 2, 0, start=True)
            between = {(1, 0): lambda: turn_x2(1), (1, 1): lambda: turn_x2(2), (2, 0): lambda: turn_x2(3),
                       (2, 1): lambda: spread_gate(0), (3, 0): lambda: spread_gate(1),
                       (NC[SH] - 1, 1): lambda: turn_in(0, 0)}
            behind = {(1, 1): ranks1, (3, 0): lambda: slots(0), (3, 1): lambda: slots(1), (4, 0): lambda: slots(2),
                      (4, 1): lambda: slots(3)}
            for k in range(1, NC[SH]):
                for s in range(2):
                    tail = k == NC[SH] - 1
                    gate_up(SH, c + k, (c + k) % 2, s, tail=tail)
                    if (k, s) in between:
                        between[k, s]()
                    if s == 0:
                        down(SH, c + k - 1, (c + k - 1) % 2, 1, start=k == 1)
                    else:
                        down(SH, c + k, (c + k) % 2, 0, stop=tail, tail=tail)
                    if (k, s) in behind:
                        behind[k, s]()

            def tile_gate_up(i, par, e):
                pe.wait_ge(t_xTs, i + 1)
                if isa(i, 2):
                    pe.wait_ge(t_hd, i - 1)
                for k in range(KH):
                    last = T.matmul(gu_ps[par], xgT[par][:, k], w1_gu[:, bass.ds((e * KH + k) * GU_N, GU_N)],
                                    start=k == 0, stop=k == KH - 1)
                last.then_inc(t_gu, 1)

            def turn_hidden(i, par):
                pe.wait_ge(t_hd, i + 1)
                if isa(i, 2):
                    pe.wait_ge(t_hTs, i - 1)
                for k in range(2):
                    last = T.transpose(hidT_ps[par][:, k * P:(k + 1) * P], t_hid[par][:, k * HALF_I:(k + 1) * HALF_I], eye)
                last.then_inc(t_hT, 1)

            def tile_down(i, par, e):
                pe.wait_ge(t_hTs, i + 1)
                if isa(i, 2):
                    pe.wait_ge(t_put, i - 1)
                for k in range(2):
                    last = T.matmul(out_ps[par], t_hidT[par][:, k], w1_dn[0:HALF_I, bass.ds((e * 2 + k) * H, H)],
                                    start=k == 0, stop=k == 1)
                last.then_inc(t_dn, 1)

            def expert(i):
                return pe.value_load(own[0:1, tile(i)], min_val=0, max_val=E1 - 1)

            def turn_base(s):
                pe.wait_ge(s_res, KH * (s + 1))
                for t in range(4):
                    for m in range(KH):
                        last = T.transpose(Y[t // 2][s][:, (t % 2) * H + m * P:(t % 2) * H + (m + 1) * P],
                                           xT[:, m, (4 * s + t) * P:(4 * s + t + 1) * P], eye)
                last.then_inc(s_bt, 1)

            def step(i, j, e, first=False, more=True):
                par = j % 2
                if not first:
                    tile_gate_up(i, par, e[2])
                if more:
                    e = e + [expert(i + 1)]
                if not first and below(i, SLOT_TILES - 1):
                    turn_in(i + 1, (j + 1) % RING)
                if isinstance(i, int) and 1 <= i < 3:
                    turn_base(i - 1)
                if isa(i, 2):
                    if isinstance(i, int) and i < 4:
                        pe.wait_ge(s_bc, KH * (i - 1))
                    tile_down(i - 2, par, e[0])
                if isa(i, 1):
                    turn_hidden(i - 1, 1 - par)
                return e[1:]

            pe.wait_ge(s_ids, 1)
            e = [None, None, expert(0)]
            pe.wait_ge(s_w1, 16 * (W1_PIECES + WD_PIECES))
            pe.wait_ge(s_prod, 2 * (C0[SH] + NC[SH]))
            tile_gate_up(0, 0, e[2])
            turn_in(1, 1)
            down(SH, c + NC[SH] - 1, (c + NC[SH] - 1) % 2, 1, stop=True, tail=True)
            body = 2 * RING
            loops = (SLOT_TILES - RING - 1) // body
            end = RING + body * loops
            held = [pe.alloc_register(f"held_expert{k}") for k in range(3)]

            def hold(e):
                for reg, v in zip(held, e):
                    pe.reg_mov(reg, v)

            def take():
                return [pe.snap(reg, min_val=0, max_val=E1 - 1) for reg in held]

            for i in range(RING):
                e = step(i, i, e, first=i == 0)
            hold(e)
            with pe.Fori(0, loops) as r:
                e = take()
                for j in range(body):
                    e = step(RING + j + body * r, j % RING, e)
                hold(e)
            e = take()
            for i in range(end, SLOT_TILES):
                e = step(i, i % RING, e, more=i < SLOT_TILES - 1)
            last = SLOT_TILES - 1
            turn_hidden(last, last % 2)
            tile_down(last - 1, (last - 1) % 2, e[0])
            tile_down(last, last % 2, e[1])


def chunks(gate, up, down):
    k, i = gate.shape
    n = i // P

    def cols(w):
        return w.reshape(k // P, P, n, P).transpose(2, 1, 0, 3).reshape(n, P, k)
    return np.ascontiguousarray(np.concatenate([cols(gate), cols(up), down.reshape(n, P, -1)], axis=2))


def on_partitions(w):
    return w.reshape(KH, P, -1).transpose(1, 0, 2)


def kernel(**inputs):
    import concourse.bacc as bacc
    from concourse.bass_utils import run_bass_kernel_spmd as run

    a = {k: np.asarray(v) for k, v in inputs.items()}
    x = a["x"].reshape(N, H)
    flat = lambda w: w.transpose(1, 0, 2).reshape(w.shape[1], -1)
    w0 = chunks(a["L0_ffn_Wg"].reshape(-1, H).T, a["L0_ffn_Wu"].reshape(-1, H).T,
                a["L0_ffn_Wd"].transpose(0, 2, 1).reshape(-1, H))
    lo_b = lambda w: w.reshape(SUBJ * RANK, -1)
    wc = chunks(np.concatenate([a["L1_cond_Wg"], lo_b(a["L1_cond_Bg"])]),
                np.concatenate([a["L1_cond_Wu"], lo_b(a["L1_cond_Bu"])]),
                np.concatenate([a["L1_cond_Wd"], flat(a["L1_cond_Ad"])], axis=1))
    sh = [a["L1_ffn_sh_" + k] for k in ("gate", "up", "down")]
    full = I_SH - SH_TAIL
    ws = chunks(sh[0][:, 0:full], sh[1][:, 0:full], sh[2][0:full])
    rest = np.zeros((1, P, WIDTH[SH]), np.float32)
    rest[0, :, 0:KH * P] = on_partitions(np.concatenate([sh[0][:, full:], sh[1][:, full:]], axis=1)).reshape(P, -1)
    rest[0, P - SH_TAIL:, 2 * KH * P:] = sh[2][full:]
    ws = np.concatenate([ws, rest])
    w1_gu = np.concatenate([a["L1_ffn_w_gate"], a["L1_ffn_w_up"]], axis=2)
    w1_gu = w1_gu.reshape(E1, KH, P, GU_N).transpose(2, 0, 1, 3).reshape(P, -1)
    w1_dn = a["L1_ffn_w_down"].reshape(E1, 2, HALF_I, H).transpose(2, 0, 1, 3).reshape(HALF_I, -1)
    la = np.stack([on_partitions(flat(a["L1_cond_Ag"])), on_partitions(flat(a["L1_cond_Au"]))], axis=2)
    small = np.concatenate([
        la.reshape(P, -1), lo_b(a["L1_cond_Bd"])], axis=1)
    routers = np.concatenate([
        on_partitions(a["L0_ffn_Wr"].T).reshape(P, -1),
        on_partitions(np.concatenate([a["L1_ffn_router_w"].T, a["L1_ffn_sh_gate_w"], np.zeros((H, 1), np.float32)],
                                     axis=1)).reshape(P, -1)], axis=1)
    cst = np.zeros((P, CS_N), np.float32)
    cst[:, CS_ID:CS_ID + P] = np.eye(P)
    cst[:, CS_TRI:CS_TRI + P] = np.triu(np.ones((P, P)))
    cst0 = np.zeros((P, CI_N), np.float32)
    cst0[:, CI_IOTA:CI_IOTA + E1] = np.arange(E1)
    cst0[np.arange(P), CI_BLK + np.arange(P) // S] = 1
    cst0[:, CI_AD] = np.arange(P) // RANK
    cst1 = np.zeros((P, CT_N), np.float32)
    cst1[:, CT_LT:CT_LT + E1 * E1] = np.tril(np.ones((E1, E1)), -1).reshape(-1)
    cst1[:, CT_THR:CT_THR + NT] = P * np.arange(NT)
    cst1[:, CT_ROW:CT_ROW + P] = np.arange(P)
    cst1[:, CT_TILE:CT_TILE + SLOT_TILES] = np.arange(SLOT_TILES)
    cst1[:, CT_TOK:CT_TOK + NT] = np.arange(N).reshape(NT, P).T + 1
    arrays = {
        "cst0": cst0, "cst1": cst1, "w1_gu": w1_gu, "w1_dn": w1_dn, "cst": cst, "idx": a["itok_B_0_7"].reshape(1, B),
        "idx_t": np.repeat(a["itok_B_0_7"].reshape(NT, BG), S, axis=1).T, "small": small, "routers": routers,
        "wsub": np.tile(a["L0_cond_weights"].transpose(1, 0, 2), (BG, 1, 1)),
        "x_tok": x.reshape(NT, P, H).transpose(1, 0, 2), "xT": on_partitions(x.T), "w0": w0, "wc": wc,
        "ws": ws,
    }
    arrays = {k: np.ascontiguousarray(v) for k, v in arrays.items()}
    nc = bacc.Bacc("TRN2", target_bir_lowering=False, num_devices=1)
    d = {k: nc.dram_tensor("in_" + k, v.shape, mybir.dt.from_np(v.dtype), kind="ExternalInput").ap()
         for k, v in arrays.items()}
    d["w"] = {L0: d["w0"], COND: d["wc"], SH: d["ws"]}
    d["scr"] = nc.dram_tensor("scr", (E0 * GPE, N), F32, kind="Internal").ap()
    d["x2"] = nc.dram_tensor("x2", (N, H), F32, kind="Internal").ap()
    d["y_b"] = nc.dram_tensor("y_b", (N, H), F32, kind="Internal").ap()
    d["out"] = nc.dram_tensor("out", (N, H), F32, kind="ExternalOutput").ap()
    build(nc, d)
    r = run(nc, [{"in_" + k: v for k, v in arrays.items()}], core_ids=[0])
    return r.results[0]["out"].reshape(B, S, H)
```

```python
from contextlib import ExitStack

import numpy as np
import concourse.bass as bass
from concourse import mybir

F32 = mybir.dt.float32
F32R = mybir.dt.float32r
BF16 = mybir.dt.bfloat16
I32 = mybir.dt.int32
U32 = mybir.dt.uint32
ALU = mybir.AluOpType
ACT = mybir.ActivationFunctionType
AX_X = mybir.AxisListType.X

P = 128
H = 256
KH = H // P
B, S = 32, 32
N = B * S
NT = N // P
HALF = N // 2
BG = P // S
SUBJ = 8
RANK = 16
I_EXP = 176
GRP = 16
GPE = I_EXP // GRP
E0, K0 = 8, 2
CAP = max(1, int(1.25 * (N * 2 / E0)))
E1, K1 = 16, 4
I_SH = 704
LOGIT1 = E1 + 2
I_COND = 1024
L0, COND, SH = 0, 1, 2
STAGES = (L0, COND, SH)
NC = {L0: E0 * I_EXP // P, COND: I_COND // P, SH: -(-I_SH // P)}
C0 = {st: sum(NC[o] for o in STAGES if o < st) for st in STAGES}
SLOT_TILES = N * K1 // P + E1 - 1
RING = 4
AHEAD = RING + 2
HALF_I = I_EXP // 2
GU_N = 2 * I_EXP
SLOT_COLS = SLOT_TILES + SLOT_TILES % 2
VALUES = 3
ROUTE_N = VALUES * SLOT_COLS
KIN = {st: KH + (st == COND) for st in STAGES}
MOUT = {st: KH + (st == COND) for st in STAGES}
WIDTH = {st: (2 * KIN[st] + MOUT[st]) * P for st in STAGES}
WMAX = max(WIDTH.values())
SH_TAIL = I_SH - (NC[SH] - 1) * P
assert 2 * SH_TAIL == P
SM_A = 0
SM_BD = SM_A + KH * 2 * P
SM_SPLIT = SM_BD + H
SM_R0 = 0
SM_R1 = SM_R0 + KH * E0
R_N = SM_R1 + KH * LOGIT1
WD_CUTS = (0, NT * ROUTE_N // (2 * H), -(-NT * (2 * ROUTE_N + SLOT_COLS) // (2 * H)), E1)
WD_EXPERTS = ((WD_CUTS[2], WD_CUTS[3]), (WD_CUTS[0], WD_CUTS[1]), (WD_CUTS[1], WD_CUTS[2]))
CS_ID, CS_TRI, CS_N = 0, P, 2 * P
CI_IOTA, CI_BLK, CI_AD = 0, E1, E1 + BG
CI_N = CI_AD + 4
CT_LT, CT_THR = 0, E1 * E1
CT_ROW = CT_THR + NT
CT_TILE = CT_ROW + P
CT_TOK = CT_TILE + SLOT_COLS
CT_N = CT_TOK + NT
W1_PIECES = NC[COND]
W1_EXP = E1 // W1_PIECES
SPLIT_EXP = 2
W1_SPLITS = E1 // SPLIT_EXP


def build(nc, d):
    with ExitStack() as ctx:
        def sb(name, shape, dt=F32):
            return ctx.enter_context(nc.sbuf_tensor(name, shape, dt))

        def sem(name):
            return ctx.enter_context(nc.semaphore(name))

        cst = sb("cst", [P, CS_N])
        cst0 = sb("cst0", [P, CI_N])
        idx_i = sb("idx_i", [P, B], I32)
        idx_f = sb("idx_f", [P, B])
        tri = sb("tri", [P, P], BF16)
        ones = sb("ones", [P, P], BF16)
        cst1 = sb("cst1", [P, CT_N])
        def sb_under(name, shape, dt):
            with nc.sbuf_tensor(name, shape, dt) as store:
                return store

        w1_raw = sb_under("w1_raw", [P, E1 * GU_N], F32)
        w1_lo = sb("w1_lo", [P, E1 * GU_N], F32R)
        w1_gu1 = sb("w1_gu1", [P, E1 * GU_N])
        oh_val_store = sb_under("oh_val_store", [P, 2 * NT * ROUTE_N], F32R)
        w1_dn = sb("w1_dn", [P, E1 * 2 * H])

        def carve(store, sizes):
            at, parts_of = 0, []
            for n in sizes:
                parts_of.append(store[:, at:at + n])
                at += n
            return parts_of
        comb_b0, comb_b1, combT, small = carve(w1_raw, [N, N, N, SM_SPLIT])
        wsel8, wblk, *prod = carve(w1_gu1, [NT * S * SUBJ, NT * P] + [HALF] * 4)
        wsel8 = wsel8.rearrange("p (t d j) -> p t d j", t=NT, d=S)
        wblk = wblk.rearrange("p (t b d) -> p t b d", t=NT, b=BG)
        comb_b = [comb_b0, comb_b1]
        x_tok, la = carve(w1_dn[:, WD_CUTS[2] * 2 * H:], [NT * H, 2 * N])
        _, oh_tile = carve(w1_dn, [2 * NT * ROUTE_N, NT * SLOT_COLS])
        x_tok = x_tok.rearrange("p (t h) -> p t h", t=NT)
        zeros = la
        la = la.rearrange("p (j n) -> p j n", j=2)
        w1_hi = sb("w1_hi", [P, E1 * GU_N], F32R)
        la_hi, la_lo, small_hi, small_lo = carve(w1_hi, [2 * N] * 2 + [SM_SPLIT] * 2)
        la_hi, la_lo = (v.rearrange("p (j n) -> p j n", j=2) for v in (la_hi, la_lo))
        routers = sb("routers", [P, R_N])
        wsub = sb("wsub", [P, SUBJ, S])
        xT = sb("xT", [P, KH, N])
        oh_row_store = sb_under("oh_row_store", [P, 2 * NT * P], F32R)
        act_f = sb("act_f", [P, KH, N])
        act_hi = sb("act_hi", [P, KH, N], F32R)
        act_lo = sb("act_lo", [P, KH, N], F32R)
        idx_ti = sb("idx_ti", [P, NT], I32)
        idx_t = sb("idx_t", [P, NT])
        subj_oh = sb("subj_oh", [P, NT, SUBJ])
        wsel = sb("wsel", [P, NT, S])
        lmask = sb("lmask", [P, B])
        r_max = sb("r_max", [P, NT])
        r_lg = sb("r_lg", [P, NT, E1 + 1])
        r_ex = sb("r_ex", [P, NT, E1 + 1])
        r_logit = sb("r_logit", [P, NT, LOGIT1])
        r_sum = sb("r_sum", [P, NT])
        r_rec = sb("r_rec", [P, NT])
        r_gate = sb("r_gate", [P, NT, E1])
        r_top = sb("r_top", [P, NT, 8])
        r_idx = sb("r_idx", [P, NT, 8], U32)
        r_idf = sb("r_idf", [P, NT, 8])
        r_oh = sb("r_oh", [P, K1, NT, E1])
        r_ohb = sb("r_ohb", [P, K0, NT, E0], BF16)
        r_kept = sb("r_kept", [P, K1, NT, E1])
        comb = sb("comb", [P, NT, E0])
        sg = sb("sg", [P, NT])
        sgT = sb("sgT", [NT, P])
        sg_b = sb("sg_b", [P, N])
        multi = sb("multi", [P, NT, E1], BF16)
        r_cmp = sb("r_cmp", [P, E1, E1])
        r_thr = sb("r_thr", [P, E1, NT])
        tiles = sb("tiles", [P, E1])
        ahead = sb("ahead", [P, E1])
        upto = sb("upto", [P, E1])
        first = sb("first", [P, E1])
        slot = sb("slot", [P, NT, E1])
        slot_k = sb("slot_k", [P, K1, NT])
        slot_i = sb("slot_i", [P, K1, NT], I32)
        tile_i = sb("tile_i", [P, K1, NT], I32)
        row_i = sb("row_i", [P, K1, NT], I32)
        tile_k = sb("tile_k", [P, K1, NT])
        row_k = sb("row_k", [P, K1, NT])
        own_cmp = sb("own_cmp", [1, SLOT_TILES, E1])
        own_f = sb("own_f", [1, SLOT_TILES])
        own = sb("own", [1, SLOT_TILES], I32)
        empty = sb("empty", [P, SLOT_TILES])
        get_f = sb("get_f", [P, SLOT_TILES])
        put_f = sb("put_f", [P, SLOT_TILES])
        slot_w = sb("slot_w", [P, SLOT_TILES])
        weight_hi = sb("weight_hi", [P, NT, K1], F32R)
        values = sb("values", [P, NT, K1, VALUES])
        get = [sb(f"get{i}", [P, 1], U32) for i in range(RING)]
        put = [sb(f"put{i}", [P, 1], U32) for i in range(RING)]
        w_raw = [sb(f"w_raw{i}", [P, WMAX]) for i in range(2)]
        w_hi = [sb(f"w_hi{i}", [P, WMAX], F32R) for i in range(2)]
        w_lo = [sb(f"w_lo{i}", [P, WMAX], F32R) for i in range(2)]
        silu = [sb(f"silu{i}", [P, HALF]) for i in range(2)]
        hid = [sb(f"hid{i}", [P, HALF]) for i in range(2)]
        hid_hi = [sb(f"hid_hi{i}", [P, HALF], F32R) for i in range(2)]
        hid_lo = [sb(f"hid_lo{i}", [P, HALF], F32R) for i in range(2)]
        oh_row = [v.rearrange("p (t r) -> p t r", t=NT) for v in carve(oh_row_store, [NT * P] * 2)]
        oh_val = [v.rearrange("p (t c) -> p t c", t=NT) for v in carve(oh_val_store, [NT * ROUTE_N] * 2)]
        oh_tile = oh_tile.rearrange("p (t c) -> p t c", t=NT)
        wide = slice(WIDTH[SH], WIDTH[SH] + H)
        xg = [w_raw[0][:, wide], w_raw[1][:, wide]] + carve(sb("xg", [P, 2 * H]), [H] * 2)
        xgT_hi = [sb(f"xgT_hi{i}", [P, P], F32R) for i in range(2)]
        xgT_lo = [sb(f"xgT_lo{i}", [P, P], F32R) for i in range(2)]
        xgT_1 = [sb(f"xgT_1{i}", [P, P]) for i in range(2)]
        t_silu = [silu[i][:, 0:I_EXP] for i in range(2)]
        t_hid = [hid[i][:, 0:I_EXP] for i in range(2)]
        t_hidT = [sb(f"t_hidT{i}", [HALF_I, 2, P]) for i in range(2)]
        t_out = [w_raw[i // 2][:, (i % 2) * H:(i % 2 + 1) * H] for i in range(RING)]
        base = act_f[:].rearrange("p k n -> p (k n)").rearrange("p (t h) -> p t h", t=NT)

        def bank(name):
            return ctx.enter_context(nc.psum_tensor(name, [P, 512], F32))
        Y = [[bank(f"y{m}{s}") for s in range(2)] for m in range(KH)]
        GU = [[bank(f"gu{s}{j}") for j in range(2)] for s in range(2)]
        HA = GU[1]
        logit_ps, rank_ps, combT_ps = GU[1][0], Y[0][1], Y[1]
        ROUTE, turn_ps = GU[1]
        at = np.cumsum([0, NT * LOGIT1, NT * E1, E1, ROUTE_N])
        logit1_ps, rank1_ps, count_ps, slot_ps = (ROUTE[:, a:b] for a, b in zip(at[:-1].tolist(), at[1:].tolist()))
        xgT_ps = [GU[1][1][:, i * H:(i + 1) * H] for i in range(2)]
        gu_ps = [GU[0][i][:, 0:GU_N] for i in range(2)]
        hidT_ps = [GU[1][0][0:HALF_I, i * H:(i + 1) * H] for i in range(2)]
        out_ps = [Y[0][i][:, 0:H] for i in range(2)]

        s_in = {k: sem("in_" + k) for k in ("cst", "idx", "small", "wsub", "xtok0", "xtok1", "xT", "cst0", "cst1", "routers", "idx_t")}
        s_raw = [sem(f"raw_landed{i}") for i in range(2)]
        s_comb = [sem(f"comb_landed{i}") for i in range(2)]
        s_scr = sem("scratch_written")
        s_zero, s_yb = sem("zeros_ready"), sem("y_b_zeroed")
        s_w1, s_w1d = sem("w1_gate_up_landed"), sem("w1_down_landed")
        s_w1h, s_w1l = sem("w1_hi_ready"), sem("w1_lo_ready")
        s_x2t, s_x2c, s_x2 = sem("x2_turned"), sem("x2_in_sbuf"), sem("x2_in_dram")
        s_ohs, s_slot, s_ids = sem("slot_onehots"), sem("slots_done"), sem("ids_ready")
        s_sgp, s_sgt = sem("sg_turned"), sem("sg_turned_sbuf")
        s_sg, s_sgb = sem("sg_in_dram"), sem("sg_spread")
        s_bt, s_bc, s_base = sem("base_turned"), sem("base_in_sbuf"), sem("base_in_out")
        t_get = sem("get_ready")
        t_in = [sem(f"tile_landed{i}") for i in range(RING)]
        t_xT, t_xTs = sem("tile_turned"), sem("tile_turned_sbuf")
        t_xh, t_xl = sem("tile_turned_hi"), sem("tile_turned_lo")
        t_gu, t_act, t_hd = sem("tile_gate_up"), sem("tile_silu"), sem("tile_hid")
        t_hT, t_hTs = sem("tile_hid_turned"), sem("tile_hid_sbuf")
        t_dn, t_put = sem("tile_down"), sem("tile_out_ready")
        s_acc = [sem("y_b_added"), sem("out_added")]
        s_held = sem("pool_held")
        s_out = sem("out_written")
        s_whi, s_whd = sem("w_hi_ready"), sem("w_hi_down_ready")
        s_wg, s_w = sem("w_gate_up_split"), sem("w_split")
        s_small = sem("small_split")
        s_g, s_u, s_d = sem("gate_done"), sem("up_done"), sem("down_done")
        s_silu, s_prod, s_h = sem("silu_done"), sem("prod_done"), sem("hid_done")
        s_hh, s_hl = sem("hid_hi_done"), sem("hid_lo_done")
        s_chain = sem("dve_chain")
        s_soh, s_ws8 = sem("subjects_ready"), sem("half_selected")
        s_blk, s_xc = sem("wblk_ready"), sem("cond0_done")
        s_x1 = sem("x1_ready")
        s_actf, s_acth, s_actl = sem("act_f_ready"), sem("act_hi_ready"), sem("act_lo_ready")
        s_cb16 = sem("consts_ready")
        s_logit, s_lgc, s_rlg, s_exp = sem("logits_done"), sem("logits_read"), sem("shifted_ready"), sem("exp_done")
        s_oh, s_rank = sem("onehot_ready"), sem("rank_done")
        s_cmb, s_cmbT, s_cmbS = sem("comb_ready"), sem("combT_done"), sem("combT_in_sbuf")
        s_la, s_lam, s_lah, s_lal = sem("lora_done"), sem("lora_masked"), sem("lora_hi"), sem("lora_lo")
        s_bd, s_ha = sem("cond_done"), sem("lora_down_done")
        s_own = sem("experts_compared")
        s_gated, s_res = sem("shared_gated"), sem("residual_out")

        block = ctx.enter_context(nc.Block())

        def half(s):
            return slice(s * HALF, (s + 1) * HALF)

        COMB0 = [16 * len({r // I_EXP for r in range(c * P, (c + 1) * P)}) for c in range(2)]

        def pair(st, n, s):
            return GU[s if st == L0 or isinstance(n, int) and n == 2 * C0[COND] + 1 else 0]

        def run_tiles(eng, step):
            body = (SLOT_TILES - RING - AHEAD) // RING
            for i in range(RING):
                step(i, i)
            with eng.Fori(0, body) as r:
                for j in range(RING):
                    step(RING + j + RING * r, j)
            for i in range(RING + RING * body, SLOT_TILES):
                step(i, i % RING)

        def gu_cols(st):
            return slice(0, 2 * KIN[st] * P)

        def split_cols(q):
            return slice(q * SPLIT_EXP * GU_N, (q + 1) * SPLIT_EXP * GU_N)

        def dn_cols(st):
            return slice(2 * KIN[st] * P, WIDTH[st])

        def select_subject(eng, t):
            dim = [P, t.stop - t.start, S, SUBJ]
            return eng.tensor_tensor(wsel8[:, t], wsub[:].rearrange("p s d -> p d s").unsqueeze(1).broadcast_to(dim),
                                     subj_oh[:, t].unsqueeze(2).broadcast_to(dim), ALU.mult)

        def rows(tail):
            return slice(SH_TAIL if tail else 0, P)

        def tile(i):
            return bass.ds(i, 1)

        def isa(i, lo):
            return not isinstance(i, int) or i >= lo

        def below(i, hi):
            return not isinstance(i, int) or i < hi

        def run_chunks(eng, st, first, last, chunk):
            pairs = (last - first) // 2
            if pairs > 1:
                with eng.Fori(0, pairs) as i:
                    for k in range(2):
                        chunk(C0[st] + first + k + 2 * i, (C0[st] + first + k) % 2)
                first += 2 * pairs
            for c in range(first, last):
                chunk(C0[st] + c, (C0[st] + c) % 2)

        def wait_pos(eng, s, v):
            if not isinstance(v, int) or v > 0:
                eng.wait_ge(s, v)

        @block.sync
        def _(sp):
            sp.dma_start(idx_ti[:], d["idx_t"]).then_inc(s_in["idx_t"], 16)
            sp.dma_start(cst0[:], d["cst0"]).then_inc(s_in["cst0"], 16)
            sp.dma_start(wsub[:], d["wsub"]).then_inc(s_in["wsub"], 16)
            sp.dma_start(x_tok[:, 0:NT // 2], d["x_tok"][:, 0:NT // 2]).then_inc(s_in["xtok0"], 16)
            sp.dma_start(x_tok[:, NT // 2:], d["x_tok"][:, NT // 2:]).then_inc(s_in["xtok1"], 16)

            def raw(st, c, par):
                wait_pos(sp, s_w, c - 1)
                sp.dma_start(w_raw[par][:, 0:WIDTH[st]], d["w"][st][bass.ds(c - C0[st], 1)]
                             .rearrange("a p n -> (a p) n")).then_inc(s_raw[par], 16)

            def raw_first(st):
                for c in range(C0[st], C0[st] + 2):
                    raw(st, c, c % 2)

            def combs(st, c, par):
                wait_pos(sp, s_h, 2 * c - 2)
                sp.dma_start(comb_b[par][:],
                             d["scr"][bass.ds((c - C0[st]) * (P // GRP), P // GRP)]
                             .unsqueeze(1).broadcast_to([P // GRP, GRP, N])).then_inc(s_comb[par], 16)

            raw_first(L0)
            sp.dma_start(idx_i[:], d["idx"].broadcast_to([P, B])).then_inc(s_in["idx"], 16)
            sp.dma_start(cst[:], d["cst"]).then_inc(s_in["cst"], 16)
            sp.dma_start(routers[:], d["routers"]).then_inc(s_in["routers"], 16)
            sp.dma_start(small, d["small"]).then_inc(s_in["small"], 16)
            for c in range(2, 4):
                raw(L0, c, c % 2)
            sp.dma_start(xT[:], d["xT"]).then_inc(s_in["xT"], 16)
            sp.wait_ge(s_cmbS, 1)
            for c in range(2):
                for e in range(E0):
                    a, b = (min(max(r - c * P, 0), P) for r in (e * I_EXP, (e + 1) * I_EXP))
                    if a < b:
                        sp.dma_start(comb_b[c][a:b], combT[e:e + 1, :].unsqueeze(1).broadcast_to([1, b - a, N])
                                     ).then_inc(s_comb[c], 16)
            sp.dma_start(d["scr"].rearrange("(e g) n -> e g n", g=GPE),
                         combT[0:E0, :].unsqueeze(1).broadcast_to([E0, GPE, N])).then_inc(s_scr, 16)
            sp.wait_ge(s_scr, 16)

            def l0_chunk(c, par):
                combs(L0, c, par)
                raw(L0, c + 2, par)
            run_chunks(sp, L0, 2, NC[L0] - 2, l0_chunk)
            for c in range(NC[L0] - 2, NC[L0]):
                combs(L0, c, c % 2)
            sp.dma_start(cst1[:], d["cst1"]).then_inc(s_in["cst1"], 16)
            sp.wait_ge(s_zero, 1)
            sp.dma_start(d["y_b"].rearrange("(p t) h -> p (t h)", p=P), zeros).then_inc(s_yb, 16)

            raw_first(COND)
            sp.wait_ge(s_h, 2 * NC[L0])

            def w1_piece(k):
                n = W1_EXP * GU_N
                for j, w in enumerate((w1_raw, w1_gu1)):
                    sp.dma_start(w[:, bass.ds(k * n, n)], d["w1_gu"][:, bass.ds(j * E1 * GU_N + k * n, n)]
                                 ).then_inc(s_w1, 16)

            def cond_chunk(c, par):
                raw(COND, c, par)
                w1_piece(c - C0[COND])
            for k in range(2):
                w1_piece(k)
            run_chunks(sp, COND, 2, NC[COND], cond_chunk)
            raw_first(SH)
            for c in range(C0[SH] + 2, C0[SH] + 4):
                raw(SH, c, c % 2)
            raw(SH, C0[SH] + 4, C0[SH] % 2)
            sp.wait_ge(s_x2c, 4)
            sp.dma_start(d["x2"].rearrange("(t p) h -> p t h", p=P), x_tok[:]).then_inc(s_x2, 16)
            sp.wait_ge(s_bd, 2)
            sp.wait_ge(s_x2, 16)

            def w1_dn_piece(k):
                w = slice(*(e * 2 * H for e in WD_EXPERTS[k]))
                sp.dma_start(w1_dn[0:HALF_I, w], d["w1_dn"][:, w]).then_inc(s_w1d, 16)
            w1_dn_piece(0)
            sp.wait_ge(s_sgt, 1)
            sp.dma_start(d["sg"].rearrange("(t p) -> t p", p=P), sgT[:]).then_inc(s_sg, 16)
            sp.wait_ge(s_sg, 16)
            sp.dma_start(sg_b[:], d["sg"].unsqueeze(0).broadcast_to([P, N])).then_inc(s_sgb, 16)
            for c in range(C0[SH] + 5, C0[SH] + NC[SH]):
                raw(SH, c, c % 2)
            sp.wait_ge(s_slot, K1 - 1)
            w1_dn_piece(1)
            sp.wait_ge(s_slot, K1)
            for j in range(2):
                sp.wait_ge(t_in[j], 16)
            w1_dn_piece(2)
            out_tok = d["out"].rearrange("(t p) h -> p t h", p=P)
            for s in range(2):
                t = slice(s * NT // 2, (s + 1) * NT // 2)
                sp.wait_ge(s_bc, KH * (s + 1))
                sp.dma_start(out_tok[:, t], base[:, t]).then_inc(s_base, 16)
            sp.wait_ge(s_out, 16)

        @block.gpsimd
        def _(pool):
            nc.gpsimd.memset(zeros, 0.0).then_inc(s_zero, 1)
            pool.wait_ge(s_in["wsub"], 16)
            pool.wait_ge(s_soh, 1)
            select_subject(nc.gpsimd, slice(NT // 2, NT)).then_inc(s_ws8, 1)

            def low(st, c, par):
                for rounded, split, w in ((s_whi, s_wg, gu_cols(st)), (s_whd, s_w, dn_cols(st))):
                    pool.wait_ge(rounded, c + 1)
                    nc.gpsimd.tensor_tensor(w_lo[par][:, w], w_raw[par][:, w], w_hi[par][:, w].bitcast(F32),
                                            ALU.subtract).then_inc(split, 1)

            low(L0, 0, 0)
            low(L0, 1, 1)
            pool.wait_ge(s_in["small"], 16)
            nc.gpsimd.tensor_copy(small_hi[:], small).then_inc(s_small, 1)
            pool.wait_ge(s_small, 1)
            nc.gpsimd.tensor_tensor(small_lo[:], small, small_hi[:].bitcast(F32),
                                    ALU.subtract).then_inc(s_small, 1)
            for st in (L0, COND):
                run_chunks(pool, st, 2 if st == L0 else 0, NC[st], lambda c, par: low(st, c, par))

            def w1_low(q):
                pool.wait_ge(s_w1h, q + 1)
                w = split_cols(q)
                nc.gpsimd.tensor_tensor(w1_lo[:, w], w1_raw[:, w], w1_hi[:, w].bitcast(F32),
                                        ALU.subtract).then_inc(s_w1l, 1)

            for k in range(NC[SH]):
                low(SH, C0[SH] + k, (C0[SH] + k) % 2)
                for q in (2 * k - 3, 2 * k - 2):
                    if 0 <= q < W1_SPLITS:
                        w1_low(q)

            def hold(sem_of, v):
                pool.wait_ge(sem_of, v)
                pool.sem_inc(s_held, 1)

            def gather(i, j):
                hold(t_get, i + 1)
                nc.gpsimd.indirect_dma_start(xg[j], None, d["x2"], bass.IndirectOffsetOnAxis(ap=get[j][:], axis=0)
                                             ).then_inc(t_in[j], 16)

            def scatter(i, j):
                par = j % 2
                hold(t_put, i + 1)
                if isa(i, 2):
                    hold(s_acc[par], 8 * (i - par))
                elif i == 1:
                    pool.wait_ge(s_base, 32)
                nc.gpsimd.indirect_dma_start((d["y_b"], d["out"])[par],
                                             bass.IndirectOffsetOnAxis(ap=put[j][:], axis=0), t_out[j], None,
                                             bounds_check=N - 1, oob_is_err=False, compute_op=ALU.add
                                             ).then_inc(s_acc[par], 16)

            def step(i, j):
                scatter(i, j)
                if below(i, SLOT_TILES - AHEAD):
                    gather(i + AHEAD, (j + AHEAD) % RING)

            pool.wait_ge(s_yb, 16)
            pool.wait_ge(s_x2, 16)
            for i in range(AHEAD):
                gather(i, i % RING)
            run_tiles(pool, step)
            pool.wait_ge(s_acc[0], 16 * ((SLOT_TILES + 1) // 2))
            pool.wait_ge(s_acc[1], 16 * (SLOT_TILES // 2))
            nc.gpsimd.dma_start(d["out"].rearrange("(p t) h -> p (t h)", p=P),
                                d["y_b"].rearrange("(p t) h -> p (t h)", p=P), accum_op=ALU.add, max_dma_last_dim=NT * H * 4
                                ).then_inc(s_out, 16)

        @block.scalar
        def _(act):
            A = nc.scalar

            def round_gate_up(st, c, par):
                act.wait_ge(s_raw[par], 8 * (c - par) + 16)
                wait_pos(act, s_d if st == COND else s_u, 2 * c - 2)
                w = gu_cols(st)
                A.activation(w_hi[par][:, w], w_raw[par][:, w], ACT.Copy).then_inc(s_whi, 1)

            def round_down(st, c, par):
                wait_pos(act, s_d, 2 * c - 2)
                w = dn_cols(st)
                A.activation(w_hi[par][:, w], w_raw[par][:, w], ACT.Copy).then_inc(s_whd, 1)

            def round_weights(st, c, par):
                round_gate_up(st, c, par)
                round_down(st, c, par)

            def silu_of(st, n, s, tail=False):
                act.wait_ge(*((s_u, n + 1) if tail else (s_g, n + 1)))
                wait_pos(act, s_prod, n - 1)
                gate = pair(st, n, s)[s if tail else 0][0:SH_TAIL if tail else P]
                A.activation(silu[s][rows(tail)], gate, ACT.Silu).then_inc(s_silu, 1)

            def hid_high(st, n, s, tail=False):
                if st == L0:
                    act.wait_ge(s_h, n + 1)
                else:
                    act.wait_ge(s_prod, n + 1)
                wait_pos(act, s_d, n - 1)
                A.activation(hid_hi[s][rows(tail)], hid[s][rows(tail)], ACT.Copy).then_inc(s_hh, 1)

            def chunk_of(st, nxt=None):
                def chunk(c, par):
                    for s in range(2):
                        silu_of(st, 2 * c + s, s)
                        hid_high(st, 2 * c + s, s)
                        if s == (nxt == COND):
                            round_weights(st if nxt is None else nxt, c + 1, 1 - par)
                return chunk

            def units(st, first):
                run_chunks(act, st, first, NC[st] - 1, chunk_of(st))
                c = C0[st] + NC[st] - 1
                chunk_of(st, st + 1)(c, c % 2)

            round_weights(L0, 0, 0)
            round_weights(L0, 1, 1)
            for s in range(2):
                act.wait_ge(s_xc, s + 1)
                for m in range(KH):
                    A.activation(act_f[:, m, half(s)], Y[m][s][:], ACT.Copy).then_inc(s_actf, 1)
            for s in range(2):
                for m in range(KH):
                    act.wait_ge(s_actf, s * KH + m + 1)
                    A.activation(act_hi[:, m, half(s)], act_f[:, m, half(s)], ACT.Copy).then_inc(s_acth, 1)
            act.wait_ge(s_rlg, 1)
            A.activation(r_ex[:, :, 0:E0], r_lg[:, :, 0:E0], ACT.Exp).then_inc(s_exp, 1)
            for n in range(4):
                silu_of(L0, n, n % 2)
                if n == 2:
                    round_gate_up(L0, 2, 0)
            for n in range(4):
                hid_high(L0, n, n % 2)
            round_down(L0, 2, 0)
            units(L0, 2)
            for s in range(2):
                for m in range(KH):
                    act.wait_ge(s_x1, s * KH + m + 1)
                    A.activation(act_hi[:, m, half(s)], xT[:, m, half(s)], ACT.Copy).then_inc(s_acth, 1)
            for s in range(2):
                for j in range(2):
                    act.wait_ge(s_lam, 2 * s + j + 1)
                    A.activation(la_hi[:, j, half(s)], la[:, j, half(s)], ACT.Copy).then_inc(s_lah, 1)
            chunk_of(COND)(C0[COND], C0[COND] % 2)
            units(COND, 1)
            for s in range(2):
                act.wait_ge(s_lam, 4 + s + 1)
                A.activation(la_hi[:, 0, half(s)], la[:, 0, half(s)], ACT.Copy).then_inc(s_lah, 1)
            for s in range(2):
                act.wait_ge(s_bd, s + 1)
                for m in range(KH):
                    A.activation(act_hi[:, m, half(s)], Y[m][s][:], ACT.Copy).then_inc(s_acth, 1)
            for s in range(2):
                for m in range(KH):
                    act.wait_ge(s_actl, 4 * KH + s * KH + m + 1)
                    A.activation(act_f[:, m, half(s)], Y[m][s][:], ACT.Copy).then_inc(s_actf, 1)
            c = C0[SH]

            def turned(b):
                act.wait_ge(s_x2t, b + 1)
                A.activation(x_tok[:, 2 * b:2 * b + 2].rearrange("p t h -> p (t h)"), turn_ps[:],
                             ACT.Copy).then_inc(s_x2c, 1)

            def turned_in(i, par):
                act.wait_ge(t_xT, i + 1)
                if isa(i, 2):
                    act.wait_ge(t_gu, i - 1)
                A.activation(xgT_hi[par][:], xgT_ps[par][:, 0:P], ACT.Copy).then_inc(t_xh, 1)
                A.activation(xgT_1[par][:], xgT_ps[par][:, P:2 * P], ACT.Copy).then_inc(t_xTs, 1)

            def w1_high(q):
                if q == 0:
                    act.wait_ge(s_w1, 16 * KH * W1_PIECES)
                w = split_cols(q)
                A.activation(w1_hi[:, w], w1_raw[:, w], ACT.Copy).then_inc(s_w1h, 1)

            for n in range(2 * NC[SH]):
                s, k = n % 2, c + n // 2
                tail = n // 2 == NC[SH] - 1
                silu_of(SH, 2 * c + n, s, tail)
                if n == 2 * NC[SH] - 1:
                    turned_in(0, 0)
                hid_high(SH, 2 * c + n, s, tail)
                if s == 0 and n // 2 + 1 < NC[SH]:
                    round_weights(SH, k + 1, (k + 1) % 2)
                if n == 0:
                    act.wait_ge(s_rlg, 2)
                    A.activation(r_ex[:], r_lg[:], ACT.Exp).then_inc(s_exp, 1)
                elif n <= 4:
                    turned(n - 1)
                elif n == 5:
                    act.wait_ge(s_sgp, 1)
                    A.activation(sgT[:], turn_ps[0:NT, 0:P], ACT.Copy).then_inc(s_sgt, 1)
                if 1 <= n <= W1_SPLITS:
                    w1_high(n - 1)

            def step(i, j):
                par = j % 2
                act.wait_ge(t_gu, i + 1)
                if isa(i, 2):
                    act.wait_ge(t_hd, i - 1)
                A.activation(t_silu[par], gu_ps[par][:, 0:I_EXP], ACT.Silu).then_inc(t_act, 1)
                if below(i, SLOT_TILES - 1):
                    turned_in(i + 1, 1 - par)
                if isinstance(i, int) and 1 <= i < 3:
                    act.wait_ge(s_bt, i)
                    for b in range(2):
                        t = (i - 1) * NT // 2 + 2 * b
                        A.activation(base[:, t:t + 2].rearrange("p t h -> p (t h)"), Y[b][i - 1][:],
                                     ACT.Copy).then_inc(s_bc, 1)

            run_tiles(act, step)

        @block.vector
        def _(dve):
            count = [0]

            def chain(ins):
                count[0] += 1
                ins.then_inc(s_chain, 1)
                dve.wait_ge(s_chain, count[0])

            V = nc.vector
            blkm = cst0[:, CI_BLK:CI_BLK + BG]
            dve.wait_ge(s_in["idx_t"], 16)
            chain(V.tensor_copy(idx_t[:], idx_ti[:]))
            dve.wait_ge(s_in["cst0"], 16)
            V.tensor_tensor(subj_oh[:], cst0[:, CI_IOTA:CI_IOTA + SUBJ].unsqueeze(1).broadcast_to([P, NT, SUBJ]),
                            idx_t[:].unsqueeze(2).broadcast_to([P, NT, SUBJ]), ALU.is_equal).then_inc(s_soh, 1)
            dve.wait_ge(s_soh, 1)
            dve.wait_ge(s_in["wsub"], 16)
            for q in range(4):
                t = slice(q * NT // 4, (q + 1) * NT // 4)
                if q < 2:
                    chain(select_subject(V, t))
                else:
                    dve.wait_ge(s_ws8, 1)
                chain(V.reduce_sum(wsel[:, t], wsel8[:, t], axis=AX_X))
                dim = [P, NT // 4, BG, S]
                V.tensor_tensor(wblk[:, t], wsel[:, t].unsqueeze(2).broadcast_to(dim),
                                blkm.unsqueeze(1).unsqueeze(3).broadcast_to(dim), ALU.mult).then_inc(s_blk, 1)
            dve.wait_ge(s_in["idx"], 16)
            chain(V.tensor_copy(idx_f[:], idx_i[:]))
            V.tensor_scalar(lmask[:], idx_f[:], cst0[:, CI_AD:CI_AD + 1], None, ALU.is_equal).then_inc(s_cb16, 1)
            dve.wait_ge(s_in["cst"], 16)
            V.tensor_copy(tri[:], cst[:, CS_TRI:CS_TRI + P]).then_inc(s_cb16, 1)
            V.memset(ones[:], 1.0).then_inc(s_cb16, 1)

            def act_low(base, src):
                for s in range(2):
                    for m in range(KH):
                        dve.wait_ge(s_acth, base + s * KH + m + 1)
                        V.tensor_tensor(act_lo[:, m, half(s)], src(m, s), act_hi[:, m, half(s)].bitcast(F32),
                                        ALU.subtract).then_inc(s_actl, 1)

            def shift(lg, ne):
                chain(V.reduce_max(r_max[:], lg, axis=AX_X))
                return V.tensor_tensor(r_lg[:, :, 0:ne], lg, r_max[:].unsqueeze(2).broadcast_to([P, NT, ne]),
                                       ALU.subtract)

            def softmax(ne, j):
                dve.wait_ge(s_exp, j)
                chain(V.reduce_sum(r_sum[:], r_ex[:, :, 0:ne], axis=AX_X))
                chain(V.reciprocal(r_rec[:], r_sum[:]))
                chain(V.tensor_tensor(r_gate[:, :, 0:ne], r_ex[:, :, 0:ne],
                                      r_rec[:].unsqueeze(2).broadcast_to([P, NT, ne]), ALU.mult))

            def top(ne, between=None):
                for t in range(NT):
                    ins = V.max(r_top[:, t, :], r_gate[:, t, 0:ne])
                chain(ins)
                if between:
                    between()
                for t in range(NT):
                    ins = V.max_index(r_idx[:, t, :], r_top[:, t, :], r_gate[:, t, 0:ne])
                chain(ins)
                chain(V.tensor_copy(r_idf[:], r_idx[:]))

            def onehot(out, ne, k):
                iota = cst0[:, CI_IOTA:CI_IOTA + ne].unsqueeze(1).broadcast_to([P, NT, ne])
                return V.tensor_tensor(out[:, k, :, 0:ne], iota,
                                       r_idf[:, :, k].unsqueeze(2).broadcast_to([P, NT, ne]), ALU.is_equal)

            def comb_out():
                for s in range(2):
                    dve.wait_ge(s_cmbT, s + 1)
                    ins = V.tensor_copy(combT[0:E0, half(s)], combT_ps[s][0:E0, :])
                ins.then_inc(s_cmbS, 1)

            def product(st, n, s, out, tail=False):
                dve.wait_ge(s_u, n + 1)
                dve.wait_ge(s_silu, n + 1)
                up = pair(st, n, s)[s if tail else 1]
                V.tensor_tensor(out[rows(tail)], silu[s][rows(tail)], up[rows(tail)], ALU.mult).then_inc(s_prod, 1)

            def weigh(st, c, par, s, src):
                dve.wait_ge(s_prod, 2 * c + s + 1)
                dve.wait_ge(s_comb[par], 8 * (c - par) + COMB0[par])
                V.tensor_tensor(hid[s][:], src[:], comb_b[par][:, half(s)], ALU.mult).then_inc(s_h, 1)

            def hid_low(n, s, tail=False):
                dve.wait_ge(s_hh, n + 1)
                wait_pos(dve, s_d, n - 1)
                V.tensor_tensor(hid_lo[s][rows(tail)], hid[s][rows(tail)], hid_hi[s][rows(tail)].bitcast(F32),
                                ALU.subtract).then_inc(s_hl, 1)

            def unit(st, c, par, s, tail=False):
                n = 2 * c + s
                product(st, n, s, prod[s] if st == L0 else hid[s], tail)
                if st == L0:
                    weigh(st, c, par, s, prod[s])
                hid_low(n, s, tail)

            def units(st, first):
                run_chunks(dve, st, first, NC[st], lambda c, par: [unit(st, c, par, s) for s in range(2)])

            act_low(0, lambda m, s: act_f[:, m, half(s)])
            dve.wait_ge(s_logit, 1)
            shift(logit_ps[:, 0:NT * E0].rearrange("p (t e) -> p t e", t=NT), E0).then_inc(s_rlg, 1)
            softmax(E0, 1)
            top(E0)
            onehot(r_ohb, E0, 0)
            onehot(r_ohb, E0, 1).then_inc(s_oh, 1)
            product(L0, 0, 0, prod[0])
            dve.wait_ge(s_oh, 1)
            dve.wait_ge(s_rank, 1)
            rank = rank_ps[:, 0:K0 * NT * E0].rearrange("p (k t e) -> p k t e", k=K0, t=NT)
            for k in range(K0):
                ins = V.scalar_tensor_tensor(out=r_kept[:, k, :, 0:E0], in0=rank[:, k], scalar=float(CAP),
                                             in1=r_ohb[:, k], op0=ALU.is_le, op1=ALU.mult)
            chain(ins)
            for k in range(K0):
                ins = V.tensor_tensor(r_oh[:, k, :, 0:E0], r_kept[:, k, :, 0:E0],
                                      r_top[:, :, k].unsqueeze(2).broadcast_to([P, NT, E0]), ALU.mult)
            chain(ins)
            V.tensor_tensor(comb[:, :, 0:E0], r_oh[:, 0, :, 0:E0], r_oh[:, 1, :, 0:E0], ALU.add).then_inc(s_cmb, 1)
            comb_out()
            product(L0, 1, 1, prod[1])
            product(L0, 2, 0, prod[2])
            for s in range(2):
                weigh(L0, 0, 0, s, prod[s])
            for s in range(2):
                hid_low(s, s)
            product(L0, 3, 1, prod[3])
            dve.wait_ge(s_hl, 2)
            for s in range(2):
                weigh(L0, 1, 1, s, prod[2 + s])
            for s in range(2):
                hid_low(2 + s, s)
            units(L0, 2)

            dve.wait_ge(s_in["xT"], 16)
            for s in range(2):
                dve.wait_ge(s_d, 2 * C0[COND] - 1 + s)
                for m in range(KH):
                    V.tensor_tensor(xT[:, m, half(s)], xT[:, m, half(s)], Y[m][s][:], ALU.add).then_inc(s_x1, 1)
                for m in range(KH):
                    dve.wait_ge(s_acth, 4 + s * KH + m + 1)
                    V.tensor_tensor(act_lo[:, m, half(s)], xT[:, m, half(s)], act_hi[:, m, half(s)].bitcast(F32),
                                    ALU.subtract).then_inc(s_actl, 1)

            dve.wait_ge(s_yb, 16)

            dve.wait_ge(s_cb16, 3)

            def keep_adapter(j, s, ps):
                mask = lmask[:, s * B // 2:(s + 1) * B // 2].unsqueeze(2).broadcast_to([P, B // 2, S])
                V.tensor_tensor(la[:, j, half(s)].rearrange("p (b t) -> p b t", t=S),
                                ps[:].rearrange("p (b t) -> p b t", t=S), mask, ALU.mult).then_inc(s_lam, 1)

            def lora_low(j, s, done):
                dve.wait_ge(s_lah, done)
                V.tensor_tensor(la_lo[:, j, half(s)], la[:, j, half(s)], la_hi[:, j, half(s)].bitcast(F32),
                                ALU.subtract).then_inc(s_lal, 1)

            for s in range(2):
                for j in range(2):
                    dve.wait_ge(s_la, 2 * s + j + 1)
                    keep_adapter(j, s, Y[j][s])
                for j in range(2):
                    lora_low(j, s, 2 * s + j + 1)
            for s in range(2):
                unit(COND, C0[COND], C0[COND] % 2, s)
            units(COND, 1)
            for s in range(2):
                dve.wait_ge(s_ha, s + 1)
                keep_adapter(0, s, HA[s])
                lora_low(0, s, 4 + s + 1)

            act_low(8, lambda m, s: Y[m][s][:])
            c = C0[SH]
            unit(SH, c, c % 2, 0)
            dve.wait_ge(s_logit, 2)
            chain(V.tensor_copy(r_logit[:], logit1_ps.rearrange("p (t e) -> p t e", t=NT)))
            V.tensor_scalar(r_lg[:, :, E1], r_logit[:, :, E1], -1.0, None, ALU.mult).then_inc(s_lgc, 1)
            shift(r_logit[:, :, 0:E1], E1).then_inc(s_rlg, 1)
            unit(SH, c, c % 2, 1)
            softmax(E1, 2)
            top(E1, between=lambda: product(SH, 2 * c + 2, 0, hid[0]))
            hid_low(2 * c + 2, 0)
            for k in range(K1):
                ins = onehot(r_oh, E1, k)
            chain(ins)
            V.tensor_tensor(r_kept[:, 0], r_oh[:, 0], r_oh[:, 1], ALU.add)
            V.reduce_sum(r_sum[:], r_top[:, :, 0:K1], axis=AX_X)
            chain(V.tensor_tensor(r_kept[:, 1], r_oh[:, 2], r_oh[:, 3], ALU.add))
            V.tensor_tensor(multi[:], r_kept[:, 0], r_kept[:, 1], ALU.add).then_inc(s_oh, 1)
            V.tensor_scalar(r_max[:], r_ex[:, :, E1], 1.0, None, ALU.add)
            chain(V.tensor_scalar(r_sum[:], r_sum[:], 1e-9, None, ALU.max))
            V.reciprocal(sg[:], r_max[:]).then_inc(s_cmb, 1)
            chain(V.reciprocal(r_rec[:], r_sum[:]))
            chain(V.tensor_tensor(r_top[:, :, 0:K1], r_top[:, :, 0:K1],
                                  r_rec[:].unsqueeze(2).broadcast_to([P, NT, K1]), ALU.mult))
            product(SH, 2 * c + 3, 1, hid[1])
            chain(V.tensor_copy(weight_hi[:], r_top[:, :, 0:K1]))
            V.tensor_copy(values[:, :, :, 0], cst1[:, CT_TOK:CT_TOK + NT].unsqueeze(2).broadcast_to([P, NT, K1]))
            V.tensor_copy(values[:, :, :, 1], weight_hi[:].bitcast(F32))
            chain(V.tensor_tensor(values[:, :, :, 2], r_top[:, :, 0:K1], weight_hi[:].bitcast(F32), ALU.subtract))
            hid_low(2 * c + 3, 1)
            dve.wait_ge(s_in["cst1"], 16)
            dve.wait_ge(s_rank, 2)
            dim = [P, E1, NT]
            chain(V.tensor_tensor(r_thr[:], count_ps.unsqueeze(2).broadcast_to(dim),
                                  cst1[:, CT_THR:CT_THR + NT].unsqueeze(1).broadcast_to(dim), ALU.is_gt))
            chain(V.reduce_sum(tiles[:], r_thr[:], axis=AX_X))
            chain(V.tensor_tensor(r_cmp[:], tiles[:].unsqueeze(1).broadcast_to([P, E1, E1]),
                                  cst1[:, CT_LT:CT_LT + E1 * E1].rearrange("p (e f) -> p e f", e=E1), ALU.mult))
            chain(V.reduce_sum(ahead[:], r_cmp[:], axis=AX_X))
            V.tensor_tensor(upto[:], ahead[:], tiles[:], ALU.add)
            chain(V.tensor_scalar(first[:], ahead[:], float(P), -1.0, ALU.mult, ALU.add))
            chain(V.tensor_tensor(slot[:], rank1_ps.rearrange("p (t e) -> p t e", t=NT),
                                  first[:].unsqueeze(1).broadcast_to([P, NT, E1]), ALU.add))
            product(SH, 2 * c + 4, 0, hid[0])
            chain(V.tensor_tensor(r_kept[:].rearrange("p k t e -> p k (t e)"), r_oh[:].rearrange("p k t e -> p k (t e)"),
                                  slot[:].rearrange("p t e -> p (t e)").unsqueeze(1).broadcast_to([P, K1, NT * E1]),
                                  ALU.mult))
            hid_low(2 * c + 4, 0)
            chain(V.reduce_sum(slot_k[:], r_kept[:], axis=AX_X))
            chain(V.tensor_copy(slot_i[:], slot_k[:]))
            shift_by = P.bit_length() - 1
            V.tensor_scalar(tile_i[:], slot_i[:], shift_by, None, ALU.arith_shift_right)
            chain(V.tensor_scalar(row_i[:], slot_i[:], P - 1, None, ALU.bitwise_and))
            V.tensor_copy(tile_k[:], tile_i[:])
            chain(V.tensor_copy(row_k[:], row_i[:]))
            dim = [1, SLOT_TILES, E1]
            V.tensor_tensor(own_cmp[:], cst1[0:1, CT_TILE:CT_TILE + SLOT_TILES].unsqueeze(2).broadcast_to(dim),
                            upto[0:1, :].unsqueeze(1).broadcast_to(dim), ALU.is_ge).then_inc(s_own, 1)

            def slot_rows(k):
                if k >= 2:
                    dve.wait_ge(s_slot, k - 1)
                V.tensor_tensor(oh_row[k % 2], cst1[:, CT_ROW:CT_ROW + P].unsqueeze(1).broadcast_to([P, NT, P]),
                                row_k[:, k].unsqueeze(2).broadcast_to([P, NT, P]), ALU.is_equal)

            def slot_values(k):
                dim = [P, NT, SLOT_COLS]
                chain(V.tensor_tensor(oh_tile, cst1[:, CT_TILE:CT_TILE + SLOT_COLS].unsqueeze(1).broadcast_to(dim),
                                      tile_k[:, k].unsqueeze(2).broadcast_to(dim), ALU.is_equal))
                dim = [P, NT, VALUES, SLOT_COLS]
                V.tensor_tensor(oh_val[k % 2].rearrange("p t (v c) -> p t v c", v=VALUES),
                                oh_tile.unsqueeze(2).broadcast_to(dim),
                                values[:, :, k].unsqueeze(3).broadcast_to(dim), ALU.mult).then_inc(s_ohs, 1)

            n = 2 * c + 5
            for k in range(K1):
                product(SH, n + k, (n + k) % 2, hid[(n + k) % 2])
                slot_rows(k)
                hid_low(n + k, (n + k) % 2)
                slot_values(k)
            product(SH, n + K1, 1, hid[1])
            dve.wait_ge(s_own, 1)
            chain(V.reduce_sum(own_f[:], own_cmp[:], axis=AX_X))
            V.tensor_scalar(own[:], own_f[:], float(E1 - 1), None, ALU.min).then_inc(s_ids, 1)
            hid_low(n + K1, 1)

            def tokens(i, j):
                if isa(i, RING):
                    dve.wait_ge(t_xT, i - RING + 1)
                V.tensor_scalar(get[j][:], get_f[:, tile(i)], 1.0, None, ALU.mult).then_inc(t_get, 1)

            dve.wait_ge(s_slot, K1)
            got = slot_ps[:, 0:SLOT_TILES]
            chain(V.tensor_scalar(get_f[:], got, -1.0, 0.0, ALU.add, ALU.max))
            for i in range(RING):
                tokens(i, i)
            V.tensor_copy(slot_w[:], slot_ps[:, SLOT_COLS:SLOT_COLS + SLOT_TILES])
            chain(V.tensor_scalar(empty[:], got, 0.0, float(4 * N), ALU.is_equal, ALU.mult))
            V.tensor_tensor(slot_w[:], slot_w[:], slot_ps[:, 2 * SLOT_COLS:2 * SLOT_COLS + SLOT_TILES], ALU.add)
            chain(V.scalar_tensor_tensor(out=put_f[:], in0=got, scalar=-1.0, in1=empty[:], op0=ALU.add, op1=ALU.add))

            def turned_low(i, par):
                dve.wait_ge(t_xTs, i + 1)
                V.tensor_tensor(xgT_lo[par][:], xgT_ps[par][:, 0:P], xgT_hi[par][:].bitcast(F32),
                                ALU.subtract).then_inc(t_xl, 1)

            c = C0[SH] + NC[SH] - 1
            product(SH, 2 * c, 0, hid[0], tail=True)
            hid_low(2 * c, 0, tail=True)
            product(SH, 2 * c + 1, 1, hid[1], tail=True)
            turned_low(0, 0)
            hid_low(2 * c + 1, 1, tail=True)

            gated = [base[:, s * NT // 2:(s + 1) * NT // 2].rearrange("p t h -> p (t h)")
                     .rearrange("p (m n) -> p m n", m=KH) for s in range(2)]

            def gate_shared(s):
                dve.wait_ge(s_sgb, 16)
                dve.wait_ge(s_d, 2 * (C0[SH] + NC[SH]) - 1 + s)
                for m in range(KH):
                    V.tensor_tensor(gated[s][:, m], Y[m][s][:], sg_b[:, half(s)], ALU.mult).then_inc(s_gated, 1)

            def add_x1(s):
                dve.wait_ge(s_gated, KH * (s + 1))
                for m in range(KH):
                    V.tensor_tensor(xT[:, m, half(s)], xT[:, m, half(s)], gated[s][:, m], ALU.add).then_inc(s_res, 1)

            gate_shared(0)

            def hidden(i, par):
                dve.wait_ge(t_act, i + 1)
                if isa(i, 2):
                    dve.wait_ge(t_hT, i - 1)
                V.tensor_tensor(t_hid[par], t_silu[par], gu_ps[par][:, I_EXP:GU_N], ALU.mult).then_inc(t_hd, 1)

            def output(i, j):
                dve.wait_ge(t_dn, i + 1)
                if isa(i, RING):
                    dve.wait_ge(s_acc[j % 2], 8 * (i - j % 2) - 16)
                V.tensor_scalar(put[j][:], put_f[:, tile(i)], 1.0, None, ALU.mult)
                V.tensor_scalar(t_out[j], out_ps[j % 2], slot_w[:, tile(i)], None, ALU.mult).then_inc(t_put, 1)

            def turned_hidden(i, par):
                dve.wait_ge(t_hT, SLOT_TILES if not below(i, SLOT_TILES - 2) else i + 1)
                if isa(i, 2):
                    dve.wait_ge(t_dn, i - 1)
                V.tensor_copy(t_hidT[par][:].rearrange("p k n -> p (k n)"), hidT_ps[par]).then_inc(t_hTs, 1)

            def step(i, j):
                hidden(i, j % 2)
                if below(i, SLOT_TILES - 1):
                    turned_low(i + 1, 1 - j % 2)
                if isinstance(i, int) and i < 2:
                    add_x1(i)
                    if i == 0:
                        gate_shared(1)
                if isa(i, 1):
                    turned_hidden(i - 1, 1 - j % 2)
                if isa(i, 2):
                    output(i - 2, (j - 2) % RING)
                if below(i, SLOT_TILES - RING):
                    tokens(i + RING, j)

            run_tiles(dve, step)
            last = SLOT_TILES - 1
            turned_hidden(last, last % 2)
            output(last - 1, (last - 1) % RING)
            output(last, last % RING)

        @block.tensor
        def _(pe):
            T = nc.tensor

            def mm3(out, w, x, start, stop):
                T.matmul(out, w[0], x[0], start=start, stop=False)
                T.matmul(out, w[0], x[1], start=False, stop=False)
                return T.matmul(out, w[1], x[0], start=False, stop=stop)

            def parts(t, *ix):
                return tuple(a[ix] for a in t)

            ACTV, SMALL, LA = (act_hi, act_lo), (small_hi, small_lo), (la_hi, la_lo)
            A = slice(None)

            for s in range(2):
                pe.wait_ge(s_in[f"xtok{s}"], 16)
                for t in range(s * NT // 2, (s + 1) * NT // 2):
                    pe.wait_ge(s_blk, t // 2 + 1)
                    for m in range(KH):
                        last = T.matmul(Y[m][s][:, (t % 4) * P:(t % 4 + 1) * P], x_tok[:, t, m * P:(m + 1) * P],
                                        wblk[:, t].rearrange("p b d -> p (b d)"), start=True, stop=True)
                last.then_inc(s_xc, 1)

            def logits(ps, done, off, ne):
                pe.wait_ge(s_in["routers"], 16)
                for t in range(NT):
                    if t % 4 == 0:
                        pe.wait_ge(s_actf, done + (t // 4 + 1) * KH)
                    for k in range(KH):
                        last = T.matmul(ps[:, t * ne:(t + 1) * ne], act_f[:, k, t * P:(t + 1) * P],
                                        routers[:, off + k * ne:off + (k + 1) * ne], start=k == 0, stop=k == KH - 1)
                last.then_inc(s_logit, 1)

            eye = cst[:, CS_ID:CS_ID + P]

            def comb_transposed():
                pe.wait_ge(s_cmb, 1)
                for t in range(NT):
                    ins = T.transpose(combT_ps[t // 4][0:E0, (t % 4) * P:(t % 4 + 1) * P], comb[:, t], eye)
                    if t % 4 == 3:
                        ins.then_inc(s_cmbT, 1)

            def ranks():
                pe.wait_ge(s_cb16, 3)
                pe.wait_ge(s_oh, 1)
                oh = r_ohb[:].rearrange("p k t e -> p (k t e)")
                total = K0 * NT * E0
                T.matmul(rank_ps[:, 0:total], tri[:], oh, start=True, stop=False)
                for b in range(1, K0 * NT):
                    last = T.matmul(rank_ps[:, b * E0:total], ones[:], oh[:, 0:total - b * E0], start=False,
                                    stop=b == K0 * NT - 1)
                last.then_inc(s_rank, 1)

            def gate_up(st, c, par, s, lora=False, between=None, tail=False):
                n, K = 2 * c + s, KIN[st]
                back = 2 if st == L0 or tail and s == 1 else 1
                if s == 0:
                    pe.wait_ge(s_wg, c + 1)
                if not (lora and s == 1):
                    wait_pos(pe, s_silu, n + 1 - back)
                    wait_pos(pe, s_prod, n + 1 - back)
                if tail:
                    for k in range(K):
                        last = mm3(GU[0][s][:], parts((w_hi[par], w_lo[par]), A, slice(k * P, (k + 1) * P)),
                                   parts(ACTV, A, k, half(s)), k == 0, k == K - 1)
                    last.then_inc(s_u, 1)
                    return
                for j, done in ((0, s_g), (1, s_u)):
                    if j and between:
                        between()
                    for k in range(K):
                        if k == KH and lora:
                            pe.wait_ge(s_lal, 2 * s + j + 1)
                        x = parts(ACTV, A, k, half(s)) if k < KH else parts(LA, A, j, half(s))
                        off = (j * K + k) * P
                        last = mm3(pair(st, n, s)[j][:], parts((w_hi[par], w_lo[par]), A, slice(off, off + P)),
                                   x, k == 0, k == K - 1)
                    last.then_inc(done, 1)

            def down(st, c, par, s, start=False, stop=False, tail=False):
                n = 2 * c + s
                if s == 0:
                    pe.wait_ge(s_w, c + 1)
                pe.wait_ge(s_hh, n + 1)
                pe.wait_ge(s_hl, n + 1)
                order = (KH, 0, 1) if stop and st == COND else range(MOUT[st])
                for m in order:
                    if start and m == KH:
                        pe.wait_ge(s_prod, 2 * C0[COND] + 2)
                    off = (2 * KIN[st] + m) * P
                    closed = stop and (st != COND or m == KH)
                    last = mm3((Y[m][s] if m < KH else HA[s])[:], parts((w_hi[par], w_lo[par]), rows(tail), slice(off, off + P)),
                               parts((hid_hi[s], hid_lo[s]), rows(tail)), start, closed)
                    if stop and m == KH:
                        last.then_inc(s_ha, 1)
                last.then_inc(s_d, 1)

            def middle(st, c, par, start=False, stop=False):
                gate_up(st, c, par, 0)
                down(st, c - 1, 1 - par, 1, start=start)
                gate_up(st, c, par, 1)
                down(st, c, par, 0, stop=stop)

            def finish(st):
                c = C0[st] + NC[st] - 1
                if st == L0:
                    for s in range(2):
                        gate_up(st, c, c % 2, s)
                    down(st, c - 1, 1 - c % 2, 1)
                    down(st, c, c % 2, 0, stop=True)
                else:
                    middle(st, c, c % 2, stop=True)
                down(st, c, c % 2, 1, stop=True)

            logits(logit_ps, 0, SM_R0, E0)
            pe.wait_ge(s_actl, KH)
            gate_up(L0, 0, 0, 0)
            pe.wait_ge(s_actl, 2 * KH)
            pe.wait_ge(s_rlg, 1)
            gate_up(L0, 0, 0, 1, between=ranks)
            comb_transposed()
            gate_up(L0, 1, 1, 0)
            gate_up(L0, 1, 1, 1)
            gate_up(L0, 2, 0, 0)
            pe.wait_ge(s_cmbS, 1)
            for c in range(2):
                for s in range(2):
                    down(L0, c, c, s, start=c == 0)
            gate_up(L0, 2, 0, 1)
            down(L0, 2, 0, 0)
            run_chunks(pe, L0, 3, NC[L0] - 1, lambda c, par: middle(L0, c, par))
            finish(L0)

            pe.wait_ge(s_small, 2)
            for s in range(2):
                for j in range(2):
                    for k in range(KH):
                        if j == 0:
                            pe.wait_ge(s_actl, 2 * KH + KH * s + k + 1)
                        off = SM_A + (k * 2 + j) * P
                        last = mm3(Y[j][s][:], parts(SMALL, A, slice(off, off + P)), parts(ACTV, A, k, half(s)),
                                   k == 0, k == KH - 1)
                    last.then_inc(s_la, 1)
            c = C0[COND]
            gate_up(COND, c, c % 2, 0, lora=True)
            gate_up(COND, c, c % 2, 1, lora=True)
            down(COND, c, c % 2, 0, start=True)
            middle(COND, c + 1, (c + 1) % 2, start=True)
            run_chunks(pe, COND, 2, NC[COND] - 1, lambda c, par: middle(COND, c, par))
            finish(COND)
            for s in range(2):
                pe.wait_ge(s_lal, 4 + s + 1)
                for m in range(KH):
                    off = SM_BD + m * P
                    last = mm3(Y[m][s][:], parts(SMALL, A, slice(off, off + P)), parts(LA, A, 0, half(s)), False, True)
                last.then_inc(s_bd, 1)

            def ranks1():
                pe.wait_ge(s_oh, 2)
                oh = multi[:].rearrange("p t e -> p (t e)")
                total = NT * E1
                T.matmul(rank1_ps, tri[:], oh, start=True, stop=False)
                for b in range(1, NT):
                    T.matmul(rank1_ps[:, b * E1:total], ones[:], oh[:, 0:total - b * E1], start=False,
                             stop=b == NT - 1)
                for b in range(NT):
                    last = T.matmul(count_ps, ones[:], oh[:, b * E1:(b + 1) * E1], start=b == 0, stop=b == NT - 1)
                last.then_inc(s_rank, 1)

            def turn_gate():
                pe.wait_ge(s_cmb, 2)
                pe.wait_ge(s_x2c, 4)
                T.transpose(turn_ps[0:NT, 0:P], sg[:], eye).then_inc(s_sgp, 1)

            def slots(k):
                pe.wait_ge(s_ohs, k + 1)
                for t in range(NT):
                    last = T.matmul(slot_ps, oh_row[k % 2][:, t], oh_val[k % 2][:, t], start=k == 0 and t == 0,
                                    stop=k == K1 - 1 and t == NT - 1)
                last.then_inc(s_slot, 1)

            def turn_x2(b):
                if b:
                    pe.wait_ge(s_x2c, b)
                for t in range(2 * b, 2 * b + 2):
                    for m in range(KH):
                        last = T.transpose(turn_ps[:, (t % 2) * H + m * P:(t % 2) * H + (m + 1) * P],
                                           act_f[:, m, t * P:(t + 1) * P], eye)
                last.then_inc(s_x2t, 1)

            def turn_in(i, j):
                par = j % 2
                pe.wait_ge(t_in[j], 4 * (i - j) + 16)
                if isa(i, 2):
                    pe.wait_ge(t_xTs, i - 1)
                    pe.wait_ge(t_xl, i - 1)
                for k in range(KH):
                    last = T.transpose(xgT_ps[par][:, k * P:(k + 1) * P], xg[j][:, k * P:(k + 1) * P], eye)
                last.then_inc(t_xT, 1)

            c = C0[SH]
            pe.wait_ge(s_actl, 5 * KH)
            gate_up(SH, c, c % 2, 0)
            pe.wait_ge(s_actl, 6 * KH)
            logits(logit1_ps, 2 * KH, SM_R1, LOGIT1)
            turn_x2(0)
            gate_up(SH, c, c % 2, 1)
            pe.wait_ge(s_actf, 4 * KH)
            down(SH, c, c % 2, 0, start=True)
            between = {(1, 0): lambda: turn_x2(1), (1, 1): lambda: turn_x2(2), (2, 0): lambda: turn_x2(3),
                       (2, 1): turn_gate}
            behind = {(1, 1): ranks1, (3, 0): lambda: slots(0), (3, 1): lambda: slots(1), (4, 0): lambda: slots(2),
                      (4, 1): lambda: slots(3)}
            for k in range(1, NC[SH] - 1):
                for s in range(2):
                    gate_up(SH, c + k, (c + k) % 2, s)
                    if (k, s) in between:
                        between[k, s]()
                    if s == 0:
                        down(SH, c + k - 1, (c + k - 1) % 2, 1, start=k == 1)
                    else:
                        down(SH, c + k, (c + k) % 2, 0)
                    if (k, s) in behind:
                        behind[k, s]()
            c += NC[SH] - 1
            for s in range(2):
                gate_up(SH, c, c % 2, s, tail=True)
            down(SH, c - 1, (c - 1) % 2, 1)
            turn_in(0, 0)
            down(SH, c, c % 2, 0, stop=True, tail=True)

            def tile_gate_up(i, par, e):
                pe.wait_ge(t_xh, i + 1)
                if isa(i, 2):
                    pe.wait_ge(t_hd, i - 1)
                w_hi, w_lo = (w[:, bass.ds(e * GU_N, GU_N)] for w in (w1_hi, w1_lo))
                T.matmul(gu_ps[par], xgT_hi[par][:], w_hi, start=True, stop=False)
                T.matmul(gu_ps[par], xgT_hi[par][:], w_lo, start=False, stop=False)
                pe.wait_ge(t_xTs, i + 1)
                T.matmul(gu_ps[par], xgT_1[par][:], w1_gu1[:, bass.ds(e * GU_N, GU_N)], start=False, stop=False)
                pe.wait_ge(t_xl, i + 1)
                T.matmul(gu_ps[par], xgT_lo[par][:], w_hi, start=False, stop=True).then_inc(t_gu, 1)

            def turn_hidden(i, par):
                pe.wait_ge(t_hd, i + 1)
                if isa(i, 2):
                    pe.wait_ge(t_hTs, i - 1)
                for k in range(2):
                    last = T.transpose(hidT_ps[par][:, k * P:(k + 1) * P], t_hid[par][:, k * HALF_I:(k + 1) * HALF_I], eye)
                last.then_inc(t_hT, 1)

            def tile_down(i, par, e):
                pe.wait_ge(t_hTs, i + 1)
                if isa(i, 2):
                    pe.wait_ge(t_put, i - 1)
                for k in range(2):
                    last = T.matmul(out_ps[par], t_hidT[par][:, k], w1_dn[0:HALF_I, bass.ds((e * 2 + k) * H, H)],
                                    start=k == 0, stop=k == 1)
                last.then_inc(t_dn, 1)

            def expert(i):
                return pe.value_load(own[0:1, tile(i)], min_val=0, max_val=E1 - 1)

            def turn_base(s):
                pe.wait_ge(s_res, KH * (s + 1))
                for t in range(4):
                    for m in range(KH):
                        last = T.transpose(Y[t // 2][s][:, (t % 2) * H + m * P:(t % 2) * H + (m + 1) * P],
                                           xT[:, m, (4 * s + t) * P:(4 * s + t + 1) * P], eye)
                last.then_inc(s_bt, 1)

            def step(i, j, e, first=False, more=True):
                par = j % 2
                if not first:
                    tile_gate_up(i, par, e[2])
                if more:
                    e = e + [expert(i + 1)]
                if not first and below(i, SLOT_TILES - 1):
                    turn_in(i + 1, (j + 1) % RING)
                if isinstance(i, int) and 1 <= i < 3:
                    turn_base(i - 1)
                if isa(i, 2):
                    if isinstance(i, int) and i == 2:
                        pe.wait_ge(s_w1d, 16 * len(WD_EXPERTS))
                    if isinstance(i, int) and i < 4:
                        pe.wait_ge(s_bc, KH * (i - 1))
                    tile_down(i - 2, par, e[0])
                if isa(i, 1):
                    turn_hidden(i - 1, 1 - par)
                return e[1:]

            pe.wait_ge(s_ids, 1)
            e = [None, None, expert(0)]
            pe.wait_ge(s_w1l, W1_SPLITS)
            pe.wait_ge(s_prod, 2 * (C0[SH] + NC[SH]) - 1)
            tile_gate_up(0, 0, e[2])
            pe.wait_ge(s_prod, 2 * (C0[SH] + NC[SH]))
            turn_in(1, 1)
            down(SH, c, c % 2, 1, stop=True, tail=True)
            body = 2 * RING
            loops = (SLOT_TILES - RING - 1) // body
            end = RING + body * loops
            held = [pe.alloc_register(f"held_expert{k}") for k in range(3)]

            def hold(e):
                for reg, v in zip(held, e):
                    pe.reg_mov(reg, v)

            def take():
                return [pe.snap(reg, min_val=0, max_val=E1 - 1) for reg in held]

            for i in range(RING):
                e = step(i, i, e, first=i == 0)
            hold(e)
            with pe.Fori(0, loops) as r:
                e = take()
                for j in range(body):
                    e = step(RING + j + body * r, j % RING, e)
                hold(e)
            e = take()
            for i in range(end, SLOT_TILES):
                e = step(i, i % RING, e, more=i < SLOT_TILES - 1)
            last = SLOT_TILES - 1
            turn_hidden(last, last % 2)
            tile_down(last - 1, (last - 1) % 2, e[0])
            tile_down(last, last % 2, e[1])


def chunks(gate, up, down):
    k, i = gate.shape
    n = i // P

    def cols(w):
        return w.reshape(k // P, P, n, P).transpose(2, 1, 0, 3).reshape(n, P, k)
    return np.ascontiguousarray(np.concatenate([cols(gate), cols(up), down.reshape(n, P, -1)], axis=2))


def on_partitions(w):
    return w.reshape(KH, P, -1).transpose(1, 0, 2)


def kernel(**inputs):
    import concourse.bacc as bacc
    from concourse.bass_utils import run_bass_kernel_spmd as run

    a = {k: np.asarray(v) for k, v in inputs.items()}
    x = a["x"].reshape(N, H)
    flat = lambda w: w.transpose(1, 0, 2).reshape(w.shape[1], -1)
    w0 = chunks(a["L0_ffn_Wg"].reshape(-1, H).T, a["L0_ffn_Wu"].reshape(-1, H).T,
                a["L0_ffn_Wd"].transpose(0, 2, 1).reshape(-1, H))
    lo_b = lambda w: w.reshape(SUBJ * RANK, -1)
    wc = chunks(np.concatenate([a["L1_cond_Wg"], lo_b(a["L1_cond_Bg"])]),
                np.concatenate([a["L1_cond_Wu"], lo_b(a["L1_cond_Bu"])]),
                np.concatenate([a["L1_cond_Wd"], flat(a["L1_cond_Ad"])], axis=1))
    sh = [a["L1_ffn_sh_" + k] for k in ("gate", "up", "down")]
    full = I_SH - SH_TAIL
    ws = chunks(sh[0][:, 0:full], sh[1][:, 0:full], sh[2][0:full])
    rest = np.zeros((1, P, WIDTH[SH]), np.float32)
    rest[0, :, 0:KH * P] = on_partitions(np.concatenate([sh[0][:, full:], sh[1][:, full:]], axis=1)).reshape(P, -1)
    rest[0, P - SH_TAIL:, 2 * KH * P:] = sh[2][full:]
    ws = np.concatenate([ws, rest])
    w1_gu = np.concatenate([a["L1_ffn_w_gate"], a["L1_ffn_w_up"]], axis=2)
    w1_gu = w1_gu.reshape(E1, KH, P, GU_N).transpose(2, 1, 0, 3).reshape(P, -1)
    w1_dn = a["L1_ffn_w_down"].reshape(E1, 2, HALF_I, H).transpose(2, 0, 1, 3).reshape(HALF_I, -1)
    la = np.stack([on_partitions(flat(a["L1_cond_Ag"])), on_partitions(flat(a["L1_cond_Au"]))], axis=2)
    small = np.concatenate([
        la.reshape(P, -1), lo_b(a["L1_cond_Bd"])], axis=1)
    routers = np.concatenate([
        on_partitions(a["L0_ffn_Wr"].T).reshape(P, -1),
        on_partitions(np.concatenate([a["L1_ffn_router_w"].T, a["L1_ffn_sh_gate_w"], np.zeros((H, 1), np.float32)],
                                     axis=1)).reshape(P, -1)], axis=1)
    cst = np.zeros((P, CS_N), np.float32)
    cst[:, CS_ID:CS_ID + P] = np.eye(P)
    cst[:, CS_TRI:CS_TRI + P] = np.triu(np.ones((P, P)))
    cst0 = np.zeros((P, CI_N), np.float32)
    cst0[:, CI_IOTA:CI_IOTA + E1] = np.arange(E1)
    cst0[np.arange(P), CI_BLK + np.arange(P) // S] = 1
    cst0[:, CI_AD] = np.arange(P) // RANK
    cst1 = np.zeros((P, CT_N), np.float32)
    cst1[:, CT_LT:CT_LT + E1 * E1] = np.tril(np.ones((E1, E1)), -1).reshape(-1)
    cst1[:, CT_THR:CT_THR + NT] = P * np.arange(NT)
    cst1[:, CT_ROW:CT_ROW + P] = np.arange(P)
    cst1[:, CT_TILE:CT_TILE + SLOT_COLS] = np.arange(SLOT_COLS)
    cst1[:, CT_TOK:CT_TOK + NT] = np.arange(N).reshape(NT, P).T + 1
    arrays = {
        "cst0": cst0, "cst1": cst1, "w1_gu": w1_gu, "w1_dn": w1_dn, "cst": cst, "idx": a["itok_B_0_7"].reshape(1, B),
        "idx_t": np.repeat(a["itok_B_0_7"].reshape(NT, BG), S, axis=1).T, "small": small, "routers": routers,
        "wsub": np.tile(a["L0_cond_weights"].transpose(1, 0, 2), (BG, 1, 1)),
        "x_tok": x.reshape(NT, P, H).transpose(1, 0, 2), "xT": on_partitions(x.T), "w0": w0, "wc": wc,
        "ws": ws,
    }
    arrays = {k: np.ascontiguousarray(v) for k, v in arrays.items()}
    nc = bacc.Bacc("TRN2", target_bir_lowering=False, num_devices=1)
    d = {k: nc.dram_tensor("in_" + k, v.shape, mybir.dt.from_np(v.dtype), kind="ExternalInput").ap()
         for k, v in arrays.items()}
    d["w"] = {L0: d["w0"], COND: d["wc"], SH: d["ws"]}
    d["scr"] = nc.dram_tensor("scr", (E0 * GPE, N), F32, kind="Internal").ap()
    d["sg"] = nc.dram_tensor("sg_tok", (N,), F32, kind="Internal").ap()
    d["x2"] = nc.dram_tensor("x2", (N, H), F32, kind="Internal").ap()
    d["y_b"] = nc.dram_tensor("y_b", (N, H), F32, kind="Internal").ap()
    d["out"] = nc.dram_tensor("out", (N, H), F32, kind="ExternalOutput").ap()
    build(nc, d)
    r = run(nc, [{"in_" + k: v for k, v in arrays.items()}], core_ids=[0])
    return r.results[0]["out"].reshape(B, S, H)
```
